# Optimizing a Trainium2 kernel written in Bass

```python
import numpy as np
import jax
import jax.numpy as jnp

def _softmax(x, axis=-1):
    return jax.nn.softmax(x, axis=axis)

def _gelu(x):
    return jax.nn.gelu(x, approximate=True)

def _silu(x):
    return jax.nn.silu(x)

def _sigmoid(x):
    return jax.nn.sigmoid(x)

def _layernorm(x, axis=-1, eps=1e-05):
    m = jnp.mean(x, axis=axis, keepdims=True)
    v = jnp.var(x, axis=axis, keepdims=True)
    return (x - m) / jnp.sqrt(v + eps)

def _scatter_add(tgt, idx, src, axis=0):
    return tgt.at[idx].add(src)

def _segment_sum(src, seg, n):
    return jax.ops.segment_sum(src, seg, n)
kernel_name = 'mk_gnn_resnorm_d2_gnn_r32_5aec2d'

def setup_inputs(seed: int=0):
    np.random.seed(seed)
    _w = jnp.asarray

    def _rec_inputs():
        import jax
        import jax.numpy as jnp
        _gk = jax.random.key(seed)
        x = -0.0005121 + 1.001 * jax.random.normal(jax.random.fold_in(_gk, 1), (50000, 64), jnp.float32)
        src = jax.random.randint(jax.random.fold_in(_gk, 2), (50000,), 0, 50000, jnp.int32)
        dst = jnp.minimum((50000 * jax.random.uniform(jax.random.fold_in(_gk, 3), (50000,)) ** 2.0).astype(jnp.int32), 49999)
        _o = jnp.argsort(dst, stable=True)
        src = src[_o]
        dst = dst[_o]
        edge_attr_64 = -9.77346e-05 + 0.999888 * jax.random.normal(jax.random.fold_in(_gk, 12), (50000, 64), jnp.float32)
        edge_weight = jax.random.uniform(jax.random.fold_in(_gk, 14), (50000,), jnp.float32, 0.0, 0.999999)
        return (x, src, dst, edge_attr_64, edge_weight)
    x, src, dst, edge_attr_64, edge_weight = _rec_inputs()

    def _L0_gnn_setup():
        import jax, jax.numpy as jnp
        import numpy as np
        N = 50000
        E = 25000
        D = 64
        key = jax.random.key(seed)
        k1, k2, k3, k4, k5, k6 = jax.random.split(key, 6)
        node_feats = jax.random.normal(k1, (N, D), dtype=jnp.float32)
        edge_feats = jax.random.normal(k2, (E, D), dtype=jnp.float32)
        src = jax.random.randint(k3, (E,), 0, N, dtype=jnp.int32)
        dst = jnp.sort(jax.random.randint(k4, (E,), 0, N, dtype=jnp.int32))
        lim = 1.0 / np.sqrt(D)
        W = jax.random.uniform(k5, (D, D), minval=-lim, maxval=lim, dtype=jnp.float32)
        b = jax.random.uniform(k6, (D,), minval=-lim, maxval=lim, dtype=jnp.float32)
        return {'node_feats': node_feats, 'edge_feats': edge_feats, 'src': src, 'dst': dst, 'W': W, 'b': b}
    _L0_gnn_all = _L0_gnn_setup()
    _L0_gnn_in = {k: v for k, v in _L0_gnn_all.items() if k in ('W', 'b')}
    del _L0_gnn_all

    def _L1_gnn_setup():
        import jax, jax.numpy as jnp
        import numpy as np
        N_NODES = 3125
        N_EDGES = 50000
        D_IN = 64
        D_OUT = 64
        key = jax.random.key(seed)
        k1, k2, k3, k4, k5 = jax.random.split(key, 5)
        x = jax.random.normal(k1, (N_NODES, D_IN), dtype=jnp.float32)
        edge_index = jax.random.randint(k2, (2, N_EDGES), 0, N_NODES, dtype=jnp.int64)
        edge_weight = jax.random.uniform(k3, (N_EDGES,), dtype=jnp.float32)
        W = jax.random.normal(k4, (D_OUT, D_IN), dtype=jnp.float32) / np.sqrt(D_IN)
        bias = jnp.zeros((D_OUT,), dtype=jnp.float32)
        prelu_w = jnp.array(0.25, dtype=jnp.float32)
        return {'x': x, 'edge_index': edge_index, 'edge_weight': edge_weight, 'W': W, 'bias': bias, 'prelu_w': prelu_w}
    _L1_gnn_all = _L1_gnn_setup()
    _L1_gnn_in = {k: v for k, v in _L1_gnn_all.items() if k in ('W', 'bias', 'prelu_w')}
    del _L1_gnn_all
    return {'x': x, 'src': src, 'dst': dst, 'edge_attr_64': edge_attr_64, 'edge_weight': edge_weight, 'L0_gnn_W': _L0_gnn_in['W'], 'L0_gnn_b': _L0_gnn_in['b'], 'L1_gnn_W': _L1_gnn_in['W'], 'L1_gnn_bias': _L1_gnn_in['bias'], 'L1_gnn_prelu_w': _L1_gnn_in['prelu_w']}

def reference(x, src, dst, edge_attr_64, edge_weight, L0_gnn_W, L0_gnn_b, L1_gnn_W, L1_gnn_bias, L1_gnn_prelu_w):
    import jax
    import jax.numpy as jnp

    def _L0_gnn_ref(node_feats, edge_feats, src, dst, W, b):
        import jax, jax.numpy as jnp
        import numpy as np
        N = 50000
        E = 25000
        D = 64
        m = node_feats[src] + edge_feats
        seg_max = jax.ops.segment_max(m, dst, num_segments=N)
        seg_max = jnp.where(jnp.isfinite(seg_max), seg_max, 0.0)
        ex = jnp.exp(m - seg_max[dst])
        denom = jax.ops.segment_sum(ex, dst, num_segments=N)
        a = ex / jnp.maximum(denom[dst], 1e-38)
        agg = jax.ops.segment_sum(m * a, dst, num_segments=N)
        out = jax.nn.relu(agg @ W.T + b) + node_feats
        return out

    def _L1_gnn_ref(x, edge_index, edge_weight, W, bias, prelu_w):
        import jax, jax.numpy as jnp
        import numpy as np
        N_NODES = 3125
        N_EDGES = 50000
        D_IN = 64
        D_OUT = 64
        N = x.shape[0]
        loop = jnp.arange(N, dtype=edge_index.dtype)
        src = jnp.concatenate([edge_index[0], loop])
        dst = jnp.concatenate([edge_index[1], loop])
        ew = jnp.concatenate([edge_weight, jnp.ones((N,), dtype=edge_weight.dtype)])
        deg = jax.ops.segment_sum(ew, dst, num_segments=N)
        dinv = jnp.where(deg > 0, jax.lax.rsqrt(jnp.maximum(deg, 1e-12)), 0.0)
        norm = dinv[src] * ew * dinv[dst]
        h = x @ W.T
        msg = h[src] * norm[:, None]
        out = jax.ops.segment_sum(msg, dst, num_segments=N) + bias
        return jnp.where(out > 0, out, prelu_w * out)
    edge_index = jnp.stack([src, dst])
    x = _layernorm(x + _L0_gnn_ref(x, edge_attr_64, src, dst, L0_gnn_W, L0_gnn_b), axis=-1)
    x = _layernorm(x + _L1_gnn_ref(x, edge_index, edge_weight, L1_gnn_W, L1_gnn_bias, L1_gnn_prelu_w), axis=-1)
    return x

_drawn_inputs = setup_inputs


def setup_inputs(seed=0):
    import zlib

    import numpy as np

    out = dict(_drawn_inputs(seed))
    spreads = {'L1_gnn_bias': (0.0, 0.1)}
    factors = {}
    for name, (base, spread) in spreads.items():
        noise = np.random.default_rng([zlib.crc32(name.encode()), seed]).standard_normal(out[name].shape)
        drawn = base * np.exp(spread * noise) if base else spread * noise
        out[name] = jnp.asarray(drawn.astype(out[name].dtype))
    for name, factor in factors.items():
        out[name] = (out[name] * factor).astype(out[name].dtype)
    return out
```

```python
import concourse.bass as bass
from concourse import mybir
import numpy as np
from contextlib import ExitStack

F32 = mybir.dt.float32
BF16 = mybir.dt.bfloat16
I32 = mybir.dt.int32
ALU = mybir.AluOpType
ACT = mybir.ActivationFunctionType
AX_X = mybir.AxisListType.X

N = 50000
E = 50000
D = 64
P = 128
BLK = 256
NB = -(-E // BLK)
NW = -(-N // BLK)
HALF_BLOCKS = NB // 2
HALF = HALF_BLOCKS * BLK
COLS = 2 * BLK
CHUNKS = HALF_BLOCKS // 2
SETS = NB // 2
STEPS = 4 * SETS
R = D + 1
PAD_NODE = NW * BLK - 1
TAIL_E = E - (NB - 1) * BLK
TAIL_N = N - (NW - 1) * BLK
BIG = 1.0e38
RING3 = 8
EPS = 1e-5


def constants():
    p = np.arange(P)
    ident = np.eye(P)
    node_of = np.zeros((P, 2, P))
    node_of[:] = (2 * p[None, :] + np.arange(2)[:, None])[None]
    shift = np.zeros((P, P))
    shift[p[:64], p[:64] + 64] = 1.0
    kept = np.concatenate([ident, node_of.reshape(P, -1), shift], 1)
    i = np.arange(HALF_BLOCKS)
    order = np.stack([4 * (i // 2) + i % 2, 4 * (i // 2) + 2 + i % 2])
    setup = np.zeros((P, STEPS + 4 * HALF_BLOCKS + 2 * NB + 2))
    setup[:, :STEPS] = np.arange(STEPS)
    at = STEPS
    for h_from in range(2):
        for h_to in range(2):
            before = order[h_from][:, None] < order[h_to][None, :]
            setup[:HALF_BLOCKS, at:at + HALF_BLOCKS] = before
            at += HALF_BLOCKS
    for h in range(2):
        setup[i, at + order[h]] = 1.0
        at += NB
    for h in range(2):
        setup[:HALF_BLOCKS, at + h] = order[h]
    return kept.astype(np.float32), setup.astype(np.float32)


def gnn_kernel(nc, x, src, dst, ef, ew, w0t, b0, w1t, b1, slope, kept_d, setup_d, out, rows_d, x1_d, hs_d):
    ctx = ExitStack()
    with ctx:
        def sb(name, shape, dt=F32):
            return ctx.enter_context(nc.sbuf_tensor(name, shape, dt))

        def sem(name):
            return ctx.enter_context(nc.semaphore(name))

        acc_t = sb("acc", [P, NW * 2 * R])
        acc = acc_t[:, :].rearrange("p (w q r) -> p w q r", q=2, r=R)
        accn = acc_t[:, :].rearrange("p (n r) -> p n r", r=R)
        kept = sb("kept", [P, 512])
        ident = kept[:, 0:128]
        node_of = kept[:, 128:384]
        shift = kept[:, 384:512]
        nident = sb("nident", [P, P])
        spread = sb("spread", [2 * CHUNKS, CHUNKS, P], BF16)
        starts = sb("starts", [P, COLS], BF16)
        rel = sb("rel", [P, 2, STEPS])
        wgt = sb("wgt", [P, 2, STEPS])
        idx = sb("idx", [P, 2 * NB], I32)
        idx_now = [sb(f"idx_now{u}", [P, 8], I32) for u in range(2)]
        emit = sb("emit", [P, 2, 2, HALF_BLOCKS])
        ewe = sb("ewe", [P, 2, 2, HALF_BLOCKS])
        wtab = sb("wtab", [1, STEPS], I32)
        jtab = sb("jtab", [1, STEPS], I32)
        endtab = sb("endtab", [1, NB], I32)
        captab = sb("captab", [1, CHUNKS + 1], I32)
        w0 = sb("w0", [P, P])
        w1 = sb("w1", [P, P])
        b0r = sb("b0r", [P, R])
        b1r = sb("b1r", [P, D])
        slo = sb("slo", [P, 1])
        dinv = sb("dinv", [P, 2 * NW])
        cap = sb("cap", [P, CHUNKS, 3])
        fixs = sb("fixs", [P, 16])
        fixrow = sb("fixrow", [P, 2 * R])
        onehot = sb("onehot", [P, 4, 2, 2 * P])
        steprow = sb("steprow", [P, 8, 2, R])
        WORK = 13350
        work = sb("work", [P, WORK])

        class Carve:
            def __init__(self, t, end):
                self.t, self.at, self.end = t, 0, end

            def take(self, cols, parts=P):
                self.at += cols
                assert self.at <= self.end
                return self.t[0:parts, self.at - cols:self.at]

        HB = HALF_BLOCKS
        cs = Carve(acc_t, NW * 2 * R)
        setc = cs.take(STEPS + 4 * HB + 2 * NB + 2)
        kf = setc[:, 0:STEPS]
        before = setc[0:HB, STEPS:STEPS + 4 * HB].rearrange("p (a b i) -> p a b i", a=2, b=2)
        place = setc[0:HB, STEPS + 4 * HB:STEPS + 4 * HB + 2 * NB].rearrange("p (h j) -> p h j", h=2)
        order = setc[0:HB, STEPS + 4 * HB + 2 * NB:]
        nat = {}
        for nm in ("dst", "nxt", "src"):
            nat[nm + "i"] = cs.take(2 * BLK, HB).bitcast(I32)
            nat[nm] = cs.take(2 * BLK, HB)
        nat["ew"] = cs.take(2 * BLK, HB)
        dadj = cs.take(2 * BLK, HB)
        curi, prei = cs.take(COLS, 2 * CHUNKS).bitcast(I32), cs.take(COLS, 2 * CHUNKS).bitcast(I32)
        cur, pre = cs.take(COLS, 2 * CHUNKS), cs.take(COLS, 2 * CHUNKS)
        oh = cs.take(2 * STEPS, HB).rearrange("p (h k) -> p h k", h=2)
        oha = cs.take(2 * STEPS, HB).rearrange("p (h k) -> p h k", h=2)
        dste = cs.take(2 * NB).rearrange("p (t h i) -> p t h i", t=2, h=2)
        nxte = cs.take(2 * NB).rearrange("p (t h i) -> p t h i", t=2, h=2)
        crm = cs.take(2 * NB).rearrange("p (t h i) -> p t h i", t=2, h=2)
        fpi = cs.take(2, HB).bitcast(I32)
        fwi = cs.take(4, HB).bitcast(I32)
        fw = cs.take(4, HB)
        cnt = cs.take(2, HB)
        sst = cs.take(2, HB)
        sen = cs.take(2, HB)
        fms = cs.take(2, HB)
        fadj = cs.take(2, HB)
        crs = cs.take(1, HB)
        n0i = cs.take(1).bitcast(I32)
        n0 = cs.take(1)
        one = cs.take(1, HB)
        sc = cs.take(16, 1)
        sci = cs.take(4, 1).bitcast(I32)
        capf = cs.take(CHUNKS + 1, 1)
        rowf = cs.take(STEPS, 1)
        rowj = cs.take(STEPS, 1)
        rowe = cs.take(NB, 1)
        crj = cs.take(2 * BLK, HB)

        ca = Carve(work, WORK)
        g1 = [ca.take(8 * D) for _ in range(2)]
        e1 = [ca.take(8 * D) for _ in range(2)]
        m_s = [ca.take(COLS) for _ in range(2)]
        msa_w = [ca.take(3 * (COLS + 1)) for _ in range(2)]
        msa = [t.rearrange("p (a c) -> p a c", a=3) for t in msa_w]
        run_max, run_den, run_sum = [[t[:, a, :] for t in msa] for a in range(3)]
        ex = [ca.take(COLS) for _ in range(2)]
        dec = [ca.take(COLS) for _ in range(2)]
        mex = [ca.take(COLS) for _ in range(2)]
        rden = [ca.take(COLS) for _ in range(2)]
        q1 = [ca.take(COLS) for _ in range(2)]
        rows_w = [ca.take(4 * 2 * R) for _ in range(2)]
        rows = [t.rearrange("p (hb t r) -> p hb t r", t=2, r=R) for t in rows_w]
        cb = Carve(work, WORK)
        xin = [cb.take(8 * D) for _ in range(2)]
        sq = [cb.take(8 * D) for _ in range(2)]
        x1s = [cb.take(8 * D) for _ in range(2)]
        xds = [cb.take(8 * D) for _ in range(2)]
        xdt = [cb.take(8 * D) for _ in range(2)]
        var, mean, rstd, rdin = [cb.take(2 * NW) for _ in range(4)]
        ring3 = cb.take(RING3 * 2 * D).rearrange("p (j t f) -> p j t f", t=2, f=D)

        bank = [ctx.enter_context(nc.psum_tensor(f"bank{i}", [P, 512], F32)) for i in range(8)]
        m_p, n_p, q_p = bank[0:2], bank[2:4], bank[4:6]

        names = """passed pads nat_d nat_s nat_w flags_d misc_d consts_d weights_d dch ppe1 ppe2 tables acc_init cst16
        tr m_ready colmax max_ready dt_ready exp_ready sum_ready mex_ready den_ready rc_ln rc_ready q_ready w_ready rows_ready
        captured fix_row fix_pe fix_q fix_a fix_store
        built mm added built3 mm3 added3
        z1 z z_sum z_mean z_cen z_sq z_var dv_a dv_b dv_c st_a st_b xd xd_t xd_tc hsp hs_acc x1m
        gathered o_sc o_b o_neg o_x o_z o_sum o_mean o_cen o_sq o_var o_out rs_a rs_b""".split()
        S = {n: sem("s_" + n) for n in names}
        s_gath = [sem(f"s_gath{u}") for u in range(2)]
        s_idx = [sem(f"s_idx{u}") for u in range(2)]
        s_ef = [sem(f"s_ef{u}") for u in range(2)]
        s_st = [sem(f"s_rows_stored{u}") for u in range(2)]
        s_rl = [sem(f"s_steprow{u}") for u in range(8)]
        s_xin = [sem(f"s_xin{u}") for u in range(2)]
        s_x1st = [sem(f"s_x1_stored{u}") for u in range(2)]
        s_hsst = [sem(f"s_hs_stored{u}") for u in range(2)]
        s_g3 = [sem(f"s_gath3_{u}") for u in range(8)]
        s_x1in = [sem(f"s_x1in{u}") for u in range(2)]
        s_outst = [sem(f"s_out_stored{u}") for u in range(2)]

        def held(eng):
            eng.sem_inc(S["passed"], 1)

        def first(c):
            return isinstance(c, int) and c < 2

        def turns(eng, body):
            for c in range(4):
                body(c, c % 2, c // 2)
            with eng.Fori(2, CHUNKS // 2) as i:
                body(2 * i, 0, i)
                body(2 * i + 1, 1, i)
            body(CHUNKS - 1, 0, CHUNKS // 2)

        def at(ap, i, n=1):
            return ap[:, bass.ds(i, n)]

        dst_h = [dst[h * HALF:min(E, (h + 1) * HALF)] for h in range(2)]

        def blocks_of(v, h, lo=0):
            base = h * HALF + lo
            full = HB if base + HB * BLK <= E else HB - 1
            main = v[base:base + full * BLK].rearrange("(i j) -> i j", j=BLK)
            rest = v[base + full * BLK:min(E, base + HB * BLK)] if full < HB else None
            return full, main, rest

        def ef_view(c, h, b):
            base = (h * HB + b) * BLK
            r0 = base + c * COLS
            return ef[bass.ds(r0, BLK), :].rearrange("(t p) f -> p t f", p=P)

        def win_view(a, b):
            return a[bass.ds(b * 4 * BLK, 4 * BLK), :].rearrange("(w p q) f -> p w (q f)", p=P, q=2)

        block = ctx.enter_context(nc.Block())

        @block.sync
        def _(sp):
            sp.dma_start(kept[:, :], kept_d).then_inc(S["consts_d"], 16)
            sp.dma_start(setc, setup_d).then_inc(S["consts_d"], 16)
            sp.wait_ge(S["pads"], 1)
            for nm, v, lo, s in (("srci", src, 0, "nat_s"), ("dsti", dst, 0, "nat_d"), ("nxti", dst, 1, "nat_d"),
                                 ("ew", ew, 0, "nat_w")):
                for h in range(2):
                    full, main, rest = blocks_of(v, h, lo)
                    sp.dma_start(nat[nm][0:full, h * BLK:(h + 1) * BLK], main).then_inc(S[s], 16)
                    if rest is not None:
                        n = rest.shape[0]
                        sp.dma_start(nat[nm][full:full + 1, h * BLK:h * BLK + n],
                                     rest.rearrange("(a n) -> a n", a=1)).then_inc(S[s], 16)
            rows97 = 2 * CHUNKS - 1
            r = E - rows97 * COLS
            sp.dma_start(curi[0:rows97, :], dst[0:rows97 * COLS].rearrange("(a n) -> a n", n=COLS)).then_inc(S["flags_d"], 16)
            sp.dma_start(curi[rows97:rows97 + 1, 0:r],
                         dst[rows97 * COLS:E].rearrange("(a n) -> a n", a=1)).then_inc(S["flags_d"], 16)
            sp.dma_start(prei[0:1, 1:COLS], dst[0:COLS - 1].rearrange("(a n) -> a n", a=1)).then_inc(S["flags_d"], 16)
            sp.dma_start(prei[1:rows97, :],
                         dst[COLS - 1:rows97 * COLS - 1].rearrange("(a n) -> a n", n=COLS)).then_inc(S["flags_d"], 16)
            sp.dma_start(prei[rows97:rows97 + 1, 0:r],
                         dst[rows97 * COLS - 1:E - 1].rearrange("(a n) -> a n", a=1)).then_inc(S["flags_d"], 16)
            sp.dma_start(fpi[1:HB, 0:1], dst[BLK - 1:BLK - 1 + (HB - 1) * BLK].rearrange("(a n) -> a n", n=BLK)[:, 0:1], allow_slow_non_contiguous=True).then_inc(S["misc_d"], 16)
            sp.dma_start(fpi[0:HB, 1:2], dst.rearrange("(a n) -> a n", n=1)[HALF - 1:HALF + (HB - 1) * BLK:BLK, :], allow_slow_non_contiguous=True).then_inc(S["misc_d"], 16)
            sp.dma_start(n0i, dst[HALF - 1:HALF].rearrange("(a n) -> a n", a=1).broadcast_to([P, 1])).then_inc(S["misc_d"], 16)
            for t, d in ((w0, w0t), (w1, w1t)):
                for h in range(2):
                    sp.dma_start(t[h * D:(h + 1) * D, h * D:(h + 1) * D], d).then_inc(S["weights_d"], 16)
            sp.dma_start(b0r[:, 0:D], b0.rearrange("(a n) -> a n", a=1).broadcast_to([P, D])).then_inc(S["weights_d"], 16)
            sp.dma_start(b1r[:, :], b1.rearrange("(a n) -> a n", a=1).broadcast_to([P, D])).then_inc(S["weights_d"], 16)
            sp.dma_start(slo[:, :], slope.broadcast_to([P, 1])).then_inc(S["weights_d"], 16)

            def load_idx(c, u):
                sp.dma_start(idx_now[u][:, :], at(idx[:, :], 8 * c, 8)).then_inc(s_idx[u], 16)

            def load_ef(c, u):
                if not first(c):
                    sp.wait_ge(S["tr"], c - 1)
                    load_idx(c, u)
                for h in range(2):
                    for b in range(2):
                        d = e1[u].rearrange("p (b t h f) -> p b t h f", b=2, t=2, h=2)[:, b, :, h, :]
                        if isinstance(c, int) and c == CHUNKS - 1 and h == 1 and b == 1:
                            r0 = (NB - 1) * BLK
                            sp.dma_start(d[0:TAIL_E, 0:1, :].rearrange("p t f -> p (t f)"), ef[r0:E, :]).then_inc(s_ef[u], 16)
                        else:
                            sp.dma_start(d, ef_view(c, h, b)).then_inc(s_ef[u], 16)

            def store_rows(c, u):
                sp.wait_ge(S["rows_ready"], c + 1)
                dview = rows_d[bass.ds(c * 4 * P, 4 * P), :].rearrange("(j p) f -> p j f", p=P)
                sp.dma_start(dview, rows_w[u].rearrange("p (j f) -> p j f", j=4)).then_inc(s_st[u], 16)

            def load_set(s, v, i):
                for n in range(4):
                    k = 4 * s + n
                    if not first(s):
                        sp.wait_ge(S["mm"], k - 7)
                    if isinstance(k, int) and k == STEPS - 1:
                        sp.wait_ge(S["fix_store"], 16)
                    if isinstance(k, int) and k == STEPS - 1:
                        j = NB
                    else:
                        held(sp)
                        j = sp.value_load(at(jtab[0:1, :], k), min_val=0, max_val=NB - 1)
                    sp.dma_start(steprow[:, 4 * v + n, :, :].rearrange("p t r -> p (t r)"),
                                 rows_d[bass.ds(j * P, P), :]).then_inc(s_rl[4 * v + n], 16)

            def turn(c, u, i):
                if not (isinstance(c, int) and c + 2 >= CHUNKS):
                    load_ef(c + 2, u)
                if not (isinstance(c, int) and c == 0):
                    store_rows(c - 1, 1 - u)
                if not first(c):
                    sp.wait_ge(s_st[u], 16 * i)
                    held(sp)
                    load_set(c - 2, u, i - 1)

            load_ef(0, 0)
            load_ef(1, 1)
            sp.wait_ge(S["tables"], 1)
            load_idx(0, 0)
            load_idx(1, 1)
            for c in range(4):
                turn(c, c % 2, c // 2)
            with sp.Fori(2, CHUNKS // 2 - 1) as i:
                turn(2 * i, 0, i)
                turn(2 * i + 1, 1, i)
            for c in range(CHUNKS - 3, CHUNKS + 1):
                turn(c, c % 2, c // 2)
            sp.wait_ge(S["fix_row"], 1)
            sp.dma_start(rows_d[NB * P:(NB + 1) * P, :], fixrow[:, :]).then_inc(S["fix_store"], 16)
            sp.wait_ge(s_st[0], 16 * (CHUNKS // 2 + 1))
            sp.wait_ge(s_st[1], 16 * (CHUNKS // 2))
            with sp.Fori((CHUNKS - 1) // 2, SETS // 2 - 1) as i:
                load_set(2 * i, 0, i)
                load_set(2 * i + 1, 1, i)
            load_set(SETS - 2, 0, SETS // 2 - 1)
            load_set(SETS - 1, 1, SETS // 2 - 1)

            def load_x(b, u):
                if not first(b):
                    sp.wait_ge(S["z"], b - 1)
                load_nodes(x, b, xin[u], s_xin[u])

            def load_nodes(a, b, t, s):
                tv = t.rearrange("p (w f) -> p w f", w=4)
                if isinstance(b, int) and b == CHUNKS - 1:
                    r0 = b * 4 * BLK
                    sp.dma_start(tv[:, 0:3, :], a[r0:r0 + 3 * BLK, :].rearrange("(w p q) f -> p w (q f)", p=P, q=2)).then_inc(s, 16)
                    sp.dma_start(tv[0:TAIL_N // 2, 3, :],
                                 a[r0 + 3 * BLK:N, :].rearrange("(p q) f -> p (q f)", q=2)).then_inc(s, 16)
                else:
                    sp.dma_start(tv, win_view(a, b)).then_inc(s, 16)

            sp.wait_ge(S["mm"], 4 * SETS)
            sp.wait_ge(S["rows_ready"], CHUNKS)
            sp.wait_ge(S["fix_row"], 1)
            turns(sp, lambda b, u, i: load_x(b, u))

            def store2(b, u, i):
                sp.wait_ge(S["x1m"], b + 1)
                sp.dma_start(win_view(x1_d, b), x1s[u].rearrange("p (w f) -> p w f", w=4)).then_inc(s_x1st[u], 16)
                sp.wait_ge(S["hs_acc"], b + 1)
                for w in range(4):
                    sp.dma_start(hs_d[bass.ds(b * 4 * BLK + w * BLK, BLK), :].rearrange("(p q) f -> p q f", q=2),
                                 acc[:, bass.ds(4 * b + w, 1), :, 0:D].rearrange("p w q f -> p (w q) f")).then_inc(s_hsst[u], 16)
            turns(sp, store2)

            load_idx(0, 0)
            load_idx(1, 1)

            def retire(c, u, i, more=True):
                for n in range(4):
                    sp.wait_ge(s_g3[4 * u + n], 32 * (i + 1))
                    sp.sem_inc(S["gathered"], 1)
                if more:
                    load_idx(c + 2, u)
            for c in range(4):
                retire(c, c % 2, c // 2)
            with sp.Fori(2, CHUNKS // 2 - 1) as i:
                retire(2 * i, 0, i)
                retire(2 * i + 1, 1, i)
            for c in range(CHUNKS - 3, CHUNKS):
                retire(c, c % 2, c // 2, c + 2 < CHUNKS)

            sp.wait_ge(S["mm3"], 4 * SETS)
            for u in range(2):
                sp.wait_ge(s_x1st[u], 16 * (CHUNKS // 2 + 1 - u))

            def load_x1(b, u, i):
                if not first(b):
                    sp.wait_ge(S["o_x"], b - 1)
                sp.dma_start(xin[u].rearrange("p (w f) -> p w f", w=4), win_view(x1_d, b)).then_inc(s_x1in[u], 16)
            turns(sp, load_x1)

            def store_out(b, u, i):
                sp.wait_ge(S["o_out"], b + 1)
                tv = x1s[u].rearrange("p (w f) -> p w f", w=4)
                if isinstance(b, int) and b == CHUNKS - 1:
                    r0 = b * 4 * BLK
                    sp.dma_start(out[r0:r0 + 3 * BLK, :].rearrange("(w p q) f -> p w (q f)", p=P, q=2), tv[:, 0:3, :]).then_inc(s_outst[u], 16)
                    sp.dma_start(out[r0 + 3 * BLK:N, :].rearrange("(p q) f -> p (q f)", q=2),
                                 tv[0:TAIL_N // 2, 3, :]).then_inc(s_outst[u], 16)
                else:
                    sp.dma_start(win_view(out, b), tv).then_inc(s_outst[u], 16)
            turns(sp, store_out)
            sp.wait_ge(s_outst[0], 16 * (CHUNKS // 2 + 2))
            sp.wait_ge(s_outst[1], 16 * (CHUNKS // 2))

        @block.gpsimd
        def _(pool):
            pool.wait_ge(S["tables"], 1)

            def gather1(c, u, i):
                pool.wait_ge(s_idx[u], 16 * (i + 1))
                if not first(c):
                    pool.wait_ge(S["tr"], c - 1)
                held(pool)
                for h in range(2):
                    for b in range(2):
                        for t in range(2):
                            n, o = (2 * h + b) * 2 + t, ((2 * b + t) * 2 + h) * D
                            nc.gpsimd.indirect_dma_start(
                                g1[u][:, o:o + D], None, x[:, :],
                                bass.IndirectOffsetOnAxis(ap=idx_now[u][:, n:n + 1], axis=0)).then_inc(s_gath[u], 16)
            turns(pool, gather1)

            def add_x(b, u, i):
                pool.wait_ge(S["z1"], b + 1)
                a = accn[:, bass.ds(8 * b, 8), 0:D]
                nc.gpsimd.tensor_tensor(a, a, xin[u].rearrange("p (n f) -> p n f", f=D), ALU.add).then_inc(S["z"], 1)
            turns(pool, add_x)
            pool.wait_ge(S["dv_c"], 1)

            def x1_mul(b, u, i):
                if not first(b):
                    pool.wait_ge(s_x1st[u], 16 * i)
                nc.gpsimd.tensor_tensor(x1s[u].rearrange("p (n f) -> p n f", f=D), accn[:, bass.ds(8 * b, 8), 0:D],
                                        rstd[:, bass.ds(8 * b, 8)].unsqueeze(2).broadcast_to([P, 8, D]), ALU.mult).then_inc(S["x1m"], 1)
            turns(pool, x1_mul)

            for u in range(2):
                pool.wait_ge(s_hsst[u], 64 * (CHUNKS // 2 + 1 - u))
                pool.wait_ge(s_x1st[u], 16 * (CHUNKS // 2 + 1 - u))

            def gather3(c, u, i):
                pool.wait_ge(s_idx[u], 16 * (CHUNKS // 2 + 1 - u + i + 1))
                for n in range(4):
                    if not first(c):
                        e = pool.value_load(at(endtab[0:1, :], 4 * c + n - 8), min_val=1, max_val=STEPS)
                        pool.wait_ge(S["mm3"], e)
                    held(pool)
                    for t in range(2):
                        nc.gpsimd.indirect_dma_start(ring3[:, 4 * u + n, t, :], None, hs_d[:, :],
                            bass.IndirectOffsetOnAxis(ap=idx_now[u][:, 2 * n + t:2 * n + t + 1], axis=0)).then_inc(s_g3[4 * u + n], 16)
            turns(pool, gather3)

            def add_bias(b):
                pool.wait_ge(S["o_sc"], b + 1)
                a = accn[:, bass.ds(8 * b, 8), 0:D]
                nc.gpsimd.tensor_tensor(a, a, b1r[:, :].unsqueeze(1).broadcast_to([P, 8, D]), ALU.add).then_inc(S["o_b"], 1)

            def add_x1(b, u, i):
                pool.wait_ge(S["o_neg"], b + 1)
                pool.wait_ge(s_x1in[u], 16 * (i + 1))
                nc.gpsimd.tensor_tensor(xds[u], xds[u], xin[u], ALU.add).then_inc(S["o_x"], 1)

            def turn4(b, u, i):
                add_bias(b)
                if not (isinstance(b, int) and b == 0):
                    add_x1(b - 1, 1 - u, i - 1 + u)
            turns(pool, turn4)
            add_x1(CHUNKS - 1, 0, CHUNKS // 2)
            pool.wait_ge(S["rs_b"], 1)

            def out_mul(b, u, i):
                if not first(b):
                    pool.wait_ge(s_outst[u], 16 * i)
                nc.gpsimd.tensor_tensor(x1s[u].rearrange("p (n f) -> p n f", f=D), accn[:, bass.ds(8 * b, 8), 0:D],
                                        rstd[:, bass.ds(8 * b, 8)].unsqueeze(2).broadcast_to([P, 8, D]), ALU.mult).then_inc(S["o_out"], 1)
            turns(pool, out_mul)

        @block.scalar
        def _(act):
            act.wait_ge(S["tables"], 1)
            act.wait_ge(S["weights_d"], 16 * 7)
            nc.scalar.activation(accn[:, :, :], b0r[:, :].unsqueeze(1).broadcast_to([P, 2 * NW, R]), ACT.Copy).then_inc(S["acc_init"], 1)

            def copy_m(c, u):
                act.wait_ge(S["tr"], c + 1)
                if not first(c):
                    act.wait_ge(S["mex_ready"], c - 1)
                nc.scalar.activation(m_s[u], m_p[u][:, :], ACT.Copy).then_inc(S["m_ready"], 1)

            def recip(c, u):
                act.wait_ge(S["den_ready"], c + 1)
                if not first(c):
                    act.wait_ge(S["q_ready"], c - 1)
                nc.scalar.activation(rden[u], run_den[u][:, 1:], ACT.Ln).then_inc(S["rc_ln"], 1)
                act.wait_ge(S["rc_ln"], c + 1)
                nc.scalar.activation(rden[u], rden[u], ACT.Exp, scale=-1.0).then_inc(S["rc_ready"], 1)

            def exps(c, u):
                act.wait_ge(S["dt_ready"], c + 1)
                if not first(c):
                    act.wait_ge(S["sum_ready"], c - 1)
                nc.scalar.activation(dec[u], n_p[u][:, :], ACT.Exp)
                nc.scalar.activation(ex[u], m_p[u][:, :], ACT.Exp).then_inc(S["exp_ready"], 1)

            def mask_rows(c, u, i):
                act.wait_ge(S["w_ready"], c + 1)
                if not first(c):
                    act.wait_ge(s_st[u], 16 * i)
                held(act)
                for h in range(2):
                    for b in range(2):
                        for t in range(2):
                            qv = q_p[u][:, ((2 * b + t) * 2 + h) * D:((2 * b + t) * 2 + h + 1) * D]
                            nc.scalar.activation(rows[u][:, 2 * h + b, t, 0:D], qv, ACT.Copy,
                                                 scale=at(emit[:, t, h, :], 2 * c + b))
                    last = nc.scalar.activation(rows[u][:, 2 * h:2 * h + 2, :, D], ewe[:, :, h, bass.ds(2 * c, 2)].rearrange("p t b -> p b t"), ACT.Copy)
                last.then_inc(S["rows_ready"], 1)

            def capture(c, u):
                act.wait_ge(S["sum_ready"], c + 1)
                held(act)
                col = act.value_load(at(captab[0:1, :], c), min_val=0, max_val=COLS - 1)
                nc.scalar.activation(cap[:, bass.ds(c, 1), :].rearrange("p c a -> p a c"), msa[u][:, :, bass.ds(1 + col, 1)], ACT.Copy).then_inc(S["captured"], 1)

            def turn(c, u, i):
                copy_m(c, u)
                if not (isinstance(c, int) and c == 0):
                    recip(c - 1, 1 - u)
                exps(c, u)
                if not (isinstance(c, int) and c == 0):
                    mask_rows(c - 1, 1 - u, i - 1 + u)
                    capture(c - 1, 1 - u)
            turns(act, turn)
            c = CHUNKS - 1
            recip(c, 0)
            mask_rows(c, 0, c // 2)
            capture(c, 0)
            act.wait_ge(S["fix_q"], 1)
            nc.scalar.activation(fixs[:, 9:11], fixs[:, 7:9], ACT.Exp).then_inc(S["fix_a"], 1)

            act.wait_ge(S["dv_a"], 1)
            nc.scalar.activation(dinv[:, :], dinv[:, :], ACT.Sqrt).then_inc(S["st_a"], 1)

            def square(b, u):
                act.wait_ge(S["z_cen"], b + 1)
                if not first(b):
                    act.wait_ge(S["z_var"], b - 1)
                held(act)
                nc.scalar.activation(sq[u].rearrange("p (n f) -> p n f", f=D), accn[:, bass.ds(8 * b, 8), 0:D], ACT.Square).then_inc(S["z_sq"], 1)
            turns(act, lambda b, u, i: square(b, u))
            act.wait_ge(S["dv_b"], 1)
            nc.scalar.activation(rstd, var[:, :], ACT.Sqrt).then_inc(S["st_b"], 1)

            def evac2(b, u, i):
                act.wait_ge(S["xd_t"], b + 1)
                if not first(b):
                    act.wait_ge(S["hsp"], b - 1)
                nc.scalar.activation(xdt[u], m_p[u][:, :], ACT.Copy).then_inc(S["xd_tc"], 1)
                act.wait_ge(S["hsp"], b + 1)
                act.wait_ge(S["x1m"], b + 1)
                act.wait_ge(S["xd"], b + 1)
                held(act)
                nc.scalar.activation(accn[:, bass.ds(8 * b, 8), 0:D], n_p[u][:, :].rearrange("p (n f) -> p n f", f=D), ACT.Copy).then_inc(S["hs_acc"], 1)
            turns(act, evac2)

            def square4(b, u):
                act.wait_ge(S["o_cen"], b + 1)
                if not first(b):
                    act.wait_ge(S["o_var"], b - 1)
                held(act)
                nc.scalar.activation(sq[u].rearrange("p (n f) -> p n f", f=D), accn[:, bass.ds(8 * b, 8), 0:D], ACT.Square).then_inc(S["o_sq"], 1)

            turns(act, lambda b, u, i: square4(b, u))
            act.wait_ge(S["rs_a"], 1)
            nc.scalar.activation(rstd, var[:, :], ACT.Sqrt).then_inc(S["st_b"], 1)

        def uslot(s, v, alone):
            if alone:
                return bank[4 * v + s][:, 0:2 * R].rearrange("p (q r) -> p q r", q=2)
            return bank[6 + s // 2][:, (s % 2) * 2 * R:(s % 2 + 1) * 2 * R].rearrange("p (q r) -> p q r", q=2)

        @block.vector
        def _(dve):
            chain = [0]

            def link(ins):
                chain[0] += 1
                ins.then_inc(S["dch"], 1)
                dve.wait_ge(S["dch"], chain[0])

            V = nc.vector
            V.memset(nat["srci"], 0)
            V.memset(nat["dsti"], PAD_NODE)
            V.memset(nat["nxti"], PAD_NODE + 1)
            V.memset(nat["ew"], 0.0)
            V.memset(curi, PAD_NODE)
            V.memset(prei, -1)
            V.memset(fpi, 0)
            V.memset(w0[:, :], 0.0)
            V.memset(w1[:, :], 0.0)
            V.memset(b0r[:, :], 1.0)
            V.memset(one, 1.0)
            V.memset(fixrow[:, :], 0.0)
            V.memset(run_max[1][:, COLS:], -BIG)
            V.memset(run_den[1][:, COLS:], 0.0)
            V.memset(run_sum[1][:, COLS:], 0.0).then_inc(S["pads"], 1)
            dve.wait_ge(S["consts_d"], 32)
            dve.wait_ge(S["nat_s"], 16 * 3)
            dve.wait_ge(S["nat_d"], 16 * 6)
            dve.wait_ge(S["nat_w"], 16 * 3)
            dve.wait_ge(S["flags_d"], 16 * 5)
            dve.wait_ge(S["misc_d"], 16 * 3)
            for nm in ("src", "dst", "nxt"):
                V.tensor_copy(nat[nm], nat[nm + "i"])
            V.tensor_copy(cur, curi)
            V.tensor_copy(pre, prei)
            V.tensor_copy(n0, n0i)
            for h in range(2):
                V.tensor_copy(spread[:, :, h * D:(h + 1) * D],
                              ident[0:2 * CHUNKS, h * CHUNKS:(h + 1) * CHUNKS].unsqueeze(2).broadcast_to([2 * CHUNKS, CHUNKS, D]))
            V.tensor_scalar(nident[:, :], ident, -1.0, None, ALU.mult)
            V.tensor_copy(fwi[:, 0:2], fpi)
            link(V.tensor_copy(fwi[:, 2:4], nat["dsti"].rearrange("p (h j) -> p h j", h=2)[:, :, BLK - 1]))
            link(V.tensor_single_scalar(fwi, fwi, 8, ALU.arith_shift_right))
            link(V.tensor_copy(fw, fwi))
            link(V.tensor_tensor(cnt, fw[:, 2:4], fw[:, 0:2], ALU.subtract))
            link(V.tensor_scalar(cnt, cnt, 1.0, None, ALU.add))
            link(V.tensor_scalar(crj[:, 0:BLK], nat["dst"][:, BLK:2 * BLK], n0[0:HB, :], 0.0, ALU.is_equal, ALU.add, accum_out=crs))
            link(V.tensor_tensor(cur, cur, pre, ALU.is_equal))
            V.tensor_scalar(starts[0:2 * CHUNKS, :], cur, -1.0, BIG, ALU.add, ALU.mult).then_inc(S["cst16"], 1)
            dve.wait_ge(S["ppe1"], 1)
            V.tensor_copy(dste.rearrange("p t h i -> p (t h i)"), bank[0][:, 0:2 * NB])
            V.tensor_copy(nxte.rearrange("p t h i -> p (t h i)"), bank[1][:, 0:2 * NB])
            for t in range(2):
                for h in range(2):
                    V.tensor_copy(idx[:, :].rearrange("p (c h b t) -> p h t c b", h=2, b=2, t=2)[:, h, t, :, :],
                                  bank[2][:, (2 * t + h) * HB:(2 * t + h + 1) * HB].rearrange("p (c b) -> p c b", b=2))
            V.tensor_copy(ewe[:, :, :, :].rearrange("p t h i -> p (t h i)"), bank[3][:, 0:2 * NB])
            V.tensor_copy(sst, bank[4][0:HB, 0:2])
            link(V.tensor_copy(sc[:, 0:1], bank[5][0:1, 0:1]))
            V.tensor_tensor(emit[:, :, :, :].rearrange("p t h i -> p (t h i)"), dste.rearrange("p t h i -> p (t h i)"),
                            nxte.rearrange("p t h i -> p (t h i)"), ALU.not_equal)
            link(V.tensor_scalar(crm[:, :, 1, :], dste[:, :, 1, :], n0, None, ALU.not_equal))
            link(V.tensor_tensor(emit[:, :, 1, :], emit[:, :, 1, :], crm[:, :, 1, :], ALU.mult))
            V.tensor_tensor(fms, fw[:, 0:2], sst, ALU.subtract)
            link(V.tensor_tensor(sen, sst, cnt, ALU.add))
            link(V.tensor_scalar(fadj, fms, -float(BLK), None, ALU.mult))
            for h in range(2):
                V.tensor_scalar(oha[:, h, :], kf[0:HB, :], sst[:, h:h + 1], None, ALU.is_ge)
                V.tensor_scalar(dadj[:, h * BLK:(h + 1) * BLK], nat["dst"][:, h * BLK:(h + 1) * BLK], fadj[:, h:h + 1], None, ALU.add)
            link(V.tensor_copy(sc[:, 1:2], n0[0:1, :]))
            for h in range(2):
                last = V.scalar_tensor_tensor(oh[:, h, :], kf[0:HB, :], sen[:, h:h + 1], oha[:, h, :], ALU.is_lt, ALU.mult)
            link(last)
            V.tensor_copy(sci[:, 0:1], n0i[0:1, :]).then_inc(S["cst16"], 1)
            dve.wait_ge(S["cst16"], 2)
            link(V.tensor_single_scalar(sci[:, 0:1], sci[:, 0:1], 8, ALU.arith_shift_right))
            V.tensor_copy(sc[:, 4:5], sci[:, 0:1])
            V.tensor_scalar(sc[:, 2:3], sc[:, 0:1], 1.0, None, ALU.is_ge)
            link(V.tensor_scalar(sc[:, 3:4], sc[:, 0:1], -1.0, 0.0, ALU.add, ALU.max))
            link(V.tensor_scalar(sc[:, 6:7], sc[:, 4:5], -float(BLK), 1.0, ALU.mult, ALU.add))
            link(V.tensor_tensor(sc[:, 5:6], sc[:, 6:7], sc[:, 1:2], ALU.add))
            link(V.tensor_tensor(sc[:, 5:6], sc[:, 5:6], sc[:, 2:3], ALU.mult))
            link(V.tensor_scalar(capf, kf[0:1, 0:CHUNKS + 1], -float(COLS), sc[:, 3:4], ALU.mult, ALU.add))
            link(V.tensor_scalar(capf, capf, 0.0, float(COLS - 1), ALU.max, ALU.min))
            V.tensor_copy(captab[:, :], capf)
            link(V.tensor_copy(sci[:, 1:2], sc[:, 3:4]))
            link(V.tensor_single_scalar(sci[:, 1:2], sci[:, 1:2], 9, ALU.arith_shift_right))
            V.tensor_copy(captab[:, CHUNKS:CHUNKS + 1], sci[:, 1:2])
            dve.wait_ge(S["ppe2"], 1)
            for t in range(2):
                V.scalar_tensor_tensor(rel[:, t, :], kf, -float(BLK), bank[t][:, 0:STEPS], ALU.mult, ALU.add)
                V.tensor_copy(wgt[:, t, :], bank[2 + t][:, 0:STEPS])
            V.tensor_tensor(rowf, bank[4][0:1, 0:STEPS], kf[0:1, :], ALU.add)
            V.tensor_copy(rowj, bank[5][0:1, 0:STEPS])
            V.tensor_copy(rowe, bank[6][0:1, 0:NB])
            link(V.tensor_scalar(sc[:, 7:8], sc[:, 5:6], -1.0, None, ALU.add))
            V.tensor_copy(rel[0:1, 0, STEPS - 1:], sc[:, 7:8])
            V.tensor_copy(rowf[:, STEPS - 1:], sc[:, 4:5])
            link(V.memset(rowj[:, STEPS - 1:], float(NB - 1)))
            V.tensor_copy(wtab[:, :], rowf)
            V.tensor_copy(jtab[:, :], rowj)
            link(V.tensor_copy(endtab[:, :], rowe))
            V.memset(sc[:, 15:16], 0.0).then_inc(S["tables"], 1)

            def build(k, n, weighted):
                mm = S["mm3"] if weighted else S["mm"]
                if not (isinstance(k, int) and k < 4):
                    dve.wait_ge(mm, k - 3)
                for t in range(2):
                    if weighted:
                        last = V.tensor_scalar(onehot[:, n, t, :], node_of, at(rel[:, t, :], k), at(wgt[:, t, :], k),
                                               ALU.is_equal, ALU.mult)
                    else:
                        last = V.tensor_scalar(onehot[:, n, t, :], node_of, at(rel[:, t, :], k), None, ALU.is_equal)
                last.then_inc(S["built3"] if weighted else S["built"], 1)

            def add(k, n, v, alone, weighted):
                dve.wait_ge(S["mm3"] if weighted else S["mm"], k + 1 if alone else k + 2 - n % 2)
                w = dve.value_load(at(wtab[0:1, :], k), min_val=0, max_val=NW - 1)
                cols = D if weighted else R
                a = acc[:, bass.ds(w, 1), :, 0:cols].rearrange("p w q r -> p (w q) r")
                added = S["added3"] if weighted else S["added"]
                if not (isinstance(k, int) and k == 0):
                    dve.wait_ge(added, k)
                V.tensor_tensor(a, a, uslot(n, v, alone)[:, :, 0:cols], ALU.add).then_inc(added, 1)

            def scan_max(c, u):
                dve.wait_ge(S["m_ready"], c + 1)
                if not (isinstance(c, int) and c == 0):
                    dve.wait_ge(S["max_ready"], c)
                if not first(c):
                    dve.wait_ge(S["dt_ready"], c - 1)
                    dve.wait_ge(S["captured"], c - 1)
                V.tensor_copy(run_max[u][:, 0:1], run_max[1 - u][:, COLS:]).then_inc(S["colmax"], 1)
                dve.wait_ge(S["colmax"], c + 1)
                V.tensor_tensor_scan(run_max[u][:, 1:], n_p[u][:, :], m_s[u], run_max[u][:, 0:1], ALU.add, ALU.max).then_inc(S["max_ready"], 1)

            def scan_sums(c, u):
                dve.wait_ge(S["exp_ready"], c + 1)
                if not first(c):
                    dve.wait_ge(S["rc_ready"], c - 1)
                if not (isinstance(c, int) and c == 0):
                    dve.wait_ge(S["sum_ready"], c)
                V.tensor_tensor_scan(run_den[u][:, 1:], dec[u], ex[u], run_den[1 - u][:, COLS:], ALU.mult, ALU.add).then_inc(S["den_ready"], 1)
                V.tensor_tensor(mex[u], m_s[u], ex[u], ALU.mult).then_inc(S["mex_ready"], 1)
                dve.wait_ge(S["mex_ready"], c + 1)
                V.tensor_tensor_scan(run_sum[u][:, 1:], dec[u], mex[u], run_sum[1 - u][:, COLS:], ALU.mult, ALU.add).then_inc(S["sum_ready"], 1)

            def quotient(c, u):
                dve.wait_ge(S["rc_ready"], c + 1)
                dve.wait_ge(S["sum_ready"], c + 1)
                if not first(c):
                    dve.wait_ge(S["w_ready"], c - 1)
                V.scalar_tensor_tensor(q1[u], rden[u], 1.0e38, run_sum[u][:, 1:], ALU.min, ALU.mult).then_inc(S["q_ready"], 1)

            def turn(c, u, i):
                scan_max(c, u)
                if isinstance(c, int) and c == 2:
                    dve.wait_ge(S["acc_init"], 1)
                if not (isinstance(c, int) and c < 3):
                    for n in range(4):
                        add(4 * (c - 3) + n, n, 1 - u, False, False)
                if not first(c):
                    for n in range(4):
                        build(4 * (c - 2) + n, n, False)
                if not (isinstance(c, int) and c == 0):
                    quotient(c - 1, 1 - u)
                scan_sums(c, u)
            for c in range(4):
                turn(c, c % 2, c // 2)
            with dve.Fori(2, CHUNKS // 2) as i:
                turn(2 * i, 0, i)
                turn(2 * i + 1, 1, i)
            turn(CHUNKS - 1, 0, CHUNKS // 2)
            c = CHUNKS
            for n in range(4):
                add(4 * (c - 3) + n, n, 0, False, False)
            for n in range(4):
                build(4 * (c - 2) + n, n, False)
            quotient(c - 1, 0)
            for n in range(4):
                add(4 * (c - 2) + n, n, 1, False, False)

            def step_loop(lo, weighted, between):
                def one_set(s, v, add_prev):
                    for n in range(4):
                        build(4 * s + n, n, weighted)
                        if add_prev:
                            add(4 * (s - 1) + n, n, 1 - v, True, weighted)
                one_set(lo, 0, False)
                one_set(lo + 1, 1, True)
                between()
                with dve.Fori(lo // 2 + 1, SETS // 2) as i:
                    one_set(2 * i, 0, True)
                    one_set(2 * i + 1, 1, True)
                for n in range(4):
                    add(4 * (SETS - 1) + n, n, 1, True, weighted)

            def fix_crossing():
                dve.wait_ge(S["captured"], CHUNKS)
                cc = dve.value_load(captab[0:1, CHUNKS:CHUNKS + 1], min_val=0, max_val=CHUNKS - 1)
                V.tensor_copy(fixs[:, 3:6], cap[:, bass.ds(cc, 1), :].rearrange("p c a -> p (c a)"))
                dve.wait_ge(S["fix_pe"], 1)
                link(V.tensor_copy(fixs[:, 0:3], bank[7][:, 400:403]))
                link(V.tensor_tensor(fixs[:, 6:7], fixs[:, 0:1], fixs[:, 3:4], ALU.max))
                V.tensor_tensor(fixs[:, 7:8], fixs[:, 0:1], fixs[:, 6:7], ALU.subtract)
                V.tensor_tensor(fixs[:, 8:9], fixs[:, 3:4], fixs[:, 6:7], ALU.subtract).then_inc(S["fix_q"], 1)
                dve.wait_ge(S["fix_a"], 1)
                V.tensor_scalar(fixs[:, 1:3], fixs[:, 1:3], fixs[:, 9:10], None, ALU.mult)
                link(V.tensor_scalar(fixs[:, 4:6], fixs[:, 4:6], fixs[:, 10:11], None, ALU.mult))
                link(V.tensor_tensor(fixs[:, 1:3], fixs[:, 1:3], fixs[:, 4:6], ALU.add))
                link(V.tensor_scalar(fixs[:, 1:2], fixs[:, 1:2], 1.0e-38, None, ALU.max))
                link(V.reciprocal(fixs[:, 1:2], fixs[:, 1:2]))
                V.tensor_tensor(fixs[:, 11:12], fixs[:, 1:2], fixs[:, 2:3], ALU.mult).then_inc(S["fix_q"], 1)
                dve.wait_ge(S["fix_pe"], 2)
                V.tensor_copy(fixrow[0:1, 0:D], bank[7][0:1, D:2 * D]).then_inc(S["fix_row"], 1)
            fix_crossing()
            step_loop(CHUNKS - 1, False, lambda: None)

            dve.wait_ge(S["added"], STEPS)
            link(V.tensor_scalar(dinv[:, :], accn[:, :, D], 1.0e-12, None, ALU.max))
            V.tensor_scalar(rdin, accn[:, :, D], 0.0, None, ALU.is_gt).then_inc(S["dv_a"], 1)

            def nrm(b):
                return accn[:, bass.ds(8 * b, 8), 0:D]

            def relu_x(b, u, i):
                dve.wait_ge(s_xin[u], 16 * (i + 1) + (16 if isinstance(b, int) and b == CHUNKS - 1 else 0))
                V.scalar_tensor_tensor(nrm(b), nrm(b), 0.0, xin[u].rearrange("p (n f) -> p n f", f=D), ALU.max, ALU.add).then_inc(S["z1"], 1)

            def centre(b, ready, summed, meaned, done):
                dve.wait_ge(ready, b + 1)
                mv = mean[:, bass.ds(8 * b, 8)]
                V.reduce_sum(mv, nrm(b), AX_X).then_inc(summed, 1)
                dve.wait_ge(summed, b + 1)
                V.tensor_scalar(mv, mv, 1.0 / D, None, ALU.mult).then_inc(meaned, 1)
                dve.wait_ge(meaned, b + 1)
                V.tensor_tensor(nrm(b), nrm(b), mv.unsqueeze(2).broadcast_to([P, 8, D]), ALU.subtract).then_inc(done, 1)

            def sum_squares(b, u, ready, done):
                dve.wait_ge(ready, b + 1)
                V.reduce_sum(var[:, bass.ds(8 * b, 8)], sq[u].rearrange("p (n f) -> p n f", f=D), AX_X).then_inc(done, 1)

            def turn2(b, u, i):
                relu_x(b, u, i)
                if not (isinstance(b, int) and b == 0):
                    centre(b - 1, S["z"], S["z_sum"], S["z_mean"], S["z_cen"])
                if not first(b):
                    sum_squares(b - 2, u, S["z_sq"], S["z_var"])
            turns(dve, turn2)
            centre(CHUNKS - 1, S["z"], S["z_sum"], S["z_mean"], S["z_cen"])
            sum_squares(CHUNKS - 2, 1, S["z_sq"], S["z_var"])
            sum_squares(CHUNKS - 1, 0, S["z_sq"], S["z_var"])
            dve.wait_ge(S["z_var"], CHUNKS)
            V.tensor_scalar(var, var, 1.0 / D, EPS, ALU.mult, ALU.add).then_inc(S["dv_b"], 1)
            dve.wait_ge(S["st_a"], 1)
            link(V.reciprocal(dinv[:, :], dinv[:, :]))
            link(V.tensor_tensor(dinv[:, :], dinv[:, :], rdin, ALU.mult))
            dve.wait_ge(S["st_b"], 1)
            link(V.reciprocal(rstd, rstd))
            link(V.tensor_tensor(rdin, rstd, dinv[:, :], ALU.mult))
            V.memset(fixs[:, 15:16], 0.0).then_inc(S["dv_c"], 1)

            def scale_d(b, u, i):
                if not first(b):
                    dve.wait_ge(S["xd_t"], b - 1)
                V.tensor_tensor(xds[u].rearrange("p (n f) -> p n f", f=D), nrm(b),
                                rdin[:, bass.ds(8 * b, 8)].unsqueeze(2).broadcast_to([P, 8, D]), ALU.mult).then_inc(S["xd"], 1)
            turns(dve, scale_d)

            for u in range(2):
                dve.wait_ge(s_hsst[u], 64 * (CHUNKS // 2 + 1 - u))
            step_loop(0, True, lambda: None)

            dve.wait_ge(S["added3"], STEPS)

            def scale_sum(b, u, i):
                V.tensor_tensor(nrm(b), nrm(b), dinv[:, bass.ds(8 * b, 8)].unsqueeze(2).broadcast_to([P, 8, D]), ALU.mult).then_inc(S["o_sc"], 1)

            def negatives(b, u):
                dve.wait_ge(S["o_b"], b + 1)
                if not first(b):
                    dve.wait_ge(S["o_z"], b - 1)
                V.tensor_scalar(xds[u].rearrange("p (n f) -> p n f", f=D), nrm(b), 0.0, slo[:, 0:1], ALU.min, ALU.mult).then_inc(S["o_neg"], 1)

            def residual(b, u):
                dve.wait_ge(S["o_x"], b + 1)
                V.scalar_tensor_tensor(nrm(b), nrm(b), 0.0, xds[u].rearrange("p (n f) -> p n f", f=D), ALU.max, ALU.add).then_inc(S["o_z"], 1)

            def turn4(b, u, i):
                scale_sum(b, u, i)
                if not (isinstance(b, int) and b == 0):
                    negatives(b - 1, 1 - u)
                if not first(b):
                    residual(b - 2, u)
                    centre(b - 2, S["o_z"], S["o_sum"], S["o_mean"], S["o_cen"])
                if not (isinstance(b, int) and b < 3):
                    sum_squares(b - 3, 1 - u, S["o_sq"], S["o_var"])
            for b in range(4):
                turn4(b, b % 2, b // 2)
            with dve.Fori(2, CHUNKS // 2) as i:
                turn4(2 * i, 0, i)
                turn4(2 * i + 1, 1, i)
            turn4(CHUNKS - 1, 0, CHUNKS // 2)
            negatives(CHUNKS - 1, 0)
            for b in (CHUNKS - 2, CHUNKS - 1):
                residual(b, b % 2)
                centre(b, S["o_z"], S["o_sum"], S["o_mean"], S["o_cen"])
            for b in (CHUNKS - 3, CHUNKS - 2, CHUNKS - 1):
                sum_squares(b, b % 2, S["o_sq"], S["o_var"])
            dve.wait_ge(S["o_var"], CHUNKS)
            V.tensor_scalar(var, var, 1.0 / D, EPS, ALU.mult, ALU.add).then_inc(S["rs_a"], 1)
            dve.wait_ge(S["st_b"], 2)
            V.reciprocal(rstd, rstd).then_inc(S["rs_b"], 1)

        @block.tensor
        def _(pe):
            T = nc.tensor
            pe.wait_ge(S["cst16"], 1)
            for bk, nm in enumerate(("dst", "nxt", "src", "ew")):
                for t in range(2):
                    for h in range(2):
                        o = (t * 2 + h) * HB
                        T.matmul(bank[bk][:, o:o + HB], nat[nm][:, h * BLK + t * P:h * BLK + (t + 1) * P], ident[0:HB, 0:HB],
                                 start=True, stop=True)
            for h in range(2):
                for hf in range(2):
                    T.matmul(bank[4][0:HB, h:h + 1], before[:, hf, h, :], cnt[:, hf:hf + 1], start=(hf == 0), stop=(hf == 1))
            T.matmul(bank[5][0:1, 0:1], crs, one, start=True, stop=True).then_inc(S["ppe1"], 1)
            pe.wait_ge(S["cst16"], 2)
            for t in range(2):
                for h in range(2):
                    T.matmul(bank[t][:, 0:STEPS], dadj[:, h * BLK + t * P:h * BLK + (t + 1) * P], oh[:, h, :], start=(h == 0), stop=(h == 1))
            for t in range(2):
                for h in range(2):
                    T.matmul(bank[2 + t][:, 0:STEPS], nat["ew"][:, h * BLK + t * P:h * BLK + (t + 1) * P], oh[:, h, :], start=(h == 0), stop=(h == 1))
            for h in range(2):
                T.matmul(bank[4][0:1, 0:STEPS], fms[:, h:h + 1], oh[:, h, :], start=(h == 0), stop=(h == 1))
            for h in range(2):
                T.matmul(bank[5][0:1, 0:STEPS], order[:, h:h + 1], oh[:, h, :], start=(h == 0), stop=(h == 1))
            for h in range(2):
                last = T.matmul(bank[6][0:1, 0:NB], sen[:, h:h + 1], place[:, h, :], start=(h == 0), stop=(h == 1))
            last.then_inc(S["ppe2"], 1)

            def step(k, n, v, alone, weighted, i):
                added, built = (S["added3"], S["built3"]) if weighted else (S["added"], S["built"])
                pe.wait_ge(built, k + 1)
                if alone:
                    if not (isinstance(k, int) and k < 8):
                        pe.wait_ge(added, k - 7)
                elif not (isinstance(k, int) and k < 4):
                    pe.wait_ge(added, 4 * (i + 0))
                if weighted:
                    j = pe.value_load(at(jtab[0:1, :], k), min_val=0, max_val=NB - 1)
                    pe.wait_ge(S["gathered"], j + 1)
                    slot = j % RING3
                u = uslot(n, v, alone)
                for q in range(2):
                    for t in range(2):
                        if weighted:
                            r = ring3[:, bass.ds(slot, 1), t, :].rearrange("p j f -> p (j f)")
                        else:
                            r = steprow[:, 4 * v + n, t, :]
                        last = T.matmul(u[:, q, 0:(D if weighted else R)], onehot[:, n, t, q * P:(q + 1) * P], r, start=(t == 0), stop=(t == 1))
                last.then_inc(S["mm3"] if weighted else S["mm"], 1)

            def transposes(c, u, i):
                pe.wait_ge(s_gath[u], 128 * (i + 1))
                pe.wait_ge(s_ef[u], 64 * (i + 1))
                if not first(c):
                    pe.wait_ge(S["exp_ready"], c - 1)
                sel = spread[:, bass.ds(c, 1), :].rearrange("k c m -> k (c m)")
                T.matmul(n_p[u][:, :], sel, starts[0:2 * CHUNKS, :], start=True, stop=True)
                for b in range(2):
                    for t in range(2):
                        o = (2 * b + t) * P
                        for a in (g1, e1):
                            last = T.matmul(m_p[u][:, o:o + P], a[u][:, o:o + P], ident, start=(o == 0 and a is g1), stop=(o == 3 * P and a is e1), skip_group_check=True)
                last.then_inc(S["tr"], 1)

            def exponents(c, u):
                pe.wait_ge(S["max_ready"], c + 1)
                T.matmul(n_p[u][:, :], ident, run_max[u][:, 0:COLS], start=False, stop=False, skip_group_check=True)
                T.matmul(n_p[u][:, :], nident[:, :], run_max[u][:, 1:], start=False, stop=True, skip_group_check=True)
                T.matmul(m_p[u][:, :], nident[:, :], run_max[u][:, 1:], start=False, stop=True, skip_group_check=True).then_inc(S["dt_ready"], 1)

            def product(c, u):
                pe.wait_ge(S["q_ready"], c + 1)
                if not first(c):
                    pe.wait_ge(S["rows_ready"], c - 1)
                for b in range(2):
                    for t in range(2):
                        o = (2 * b + t) * P
                        last = T.matmul(q_p[u][:, o:o + P], q1[u][:, o:o + P], w0[:, :], start=True, stop=True)
                last.then_inc(S["w_ready"], 1)

            def steps(s, v, i, alone=False, weighted=False):
                for n in range(4):
                    if not weighted:
                        pe.wait_ge(s_rl[4 * v + n], 16 * (i + 1))
                    step(4 * s + n, n, v, alone, weighted, s)

            def turn(c, u, i):
                transposes(c, u, i)
                exponents(c, u)
                if not (isinstance(c, int) and c == 0):
                    product(c - 1, 1 - u)
                if not first(c):
                    steps(c - 2, u, i - 1)
            pe.wait_ge(S["tables"], 1)
            pe.wait_ge(S["weights_d"], 16 * 7)
            turns(pe, turn)
            product(CHUNKS - 1, 0)
            steps(CHUNKS - 2, 1, CHUNKS // 2 - 1)
            pe.wait_ge(S["added"], 4 * (CHUNKS - 1))
            pe.wait_ge(S["sum_ready"], CHUNKS)
            T.matmul(bank[7][:, 400:403], shift, msa[0][:, :, COLS], start=True, stop=True).then_inc(S["fix_pe"], 1)
            pe.wait_ge(S["fix_q"], 2)
            T.matmul(bank[7][0:1, 0:P], fixs[:, 11:12], w0[:, :], start=True, stop=True).then_inc(S["fix_pe"], 1)
            pe.wait_ge(S["fix_row"], 1)
            pe.wait_ge(S["rows_ready"], CHUNKS)
            lo = CHUNKS - 1
            with pe.Fori(lo // 2, SETS // 2) as i:
                steps(2 * i, 0, i, alone=True)
                steps(2 * i + 1, 1, i, alone=True)

            pe.wait_ge(S["added"], STEPS)

            def product2(b, u, i):
                pe.wait_ge(S["xd"], b + 1)
                if not first(b):
                    pe.wait_ge(S["xd_tc"], b - 1)
                for w in range(4):
                    last = T.matmul(m_p[u][:, w * P:(w + 1) * P], xds[u][:, w * P:(w + 1) * P], ident, start=True, stop=True)
                last.then_inc(S["xd_t"], 1)
                pe.wait_ge(S["xd_tc"], b + 1)
                if not first(b):
                    pe.wait_ge(S["hs_acc"], b - 1)
                for w in range(4):
                    last = T.matmul(n_p[u][:, w * P:(w + 1) * P], xdt[u][:, w * P:(w + 1) * P], w1[:, :], start=True, stop=True)
                last.then_inc(S["hsp"], 1)
            turns(pe, product2)

            pe.wait_ge(S["hs_acc"], CHUNKS)
            steps(0, 0, 0, True, True)
            steps(1, 1, 0, True, True)
            with pe.Fori(1, SETS // 2) as i:
                steps(2 * i, 0, i, True, True)
                steps(2 * i + 1, 1, i, True, True)


def kernel(x, src, dst, edge_attr_64, edge_weight, L0_gnn_W, L0_gnn_b, L1_gnn_W, L1_gnn_bias, L1_gnn_prelu_w):
    import concourse.bacc as bacc
    from concourse.bass_utils import run_bass_kernel_spmd

    kept, setup = constants()
    arrays = {
        "x": np.asarray(x), "src": np.asarray(src), "dst": np.asarray(dst),
        "ef": np.asarray(edge_attr_64), "ew": np.asarray(edge_weight),
        "w0t": np.ascontiguousarray(np.asarray(L0_gnn_W).T), "b0": np.asarray(L0_gnn_b),
        "w1t": np.ascontiguousarray(np.asarray(L1_gnn_W).T), "b1": np.asarray(L1_gnn_bias),
        "slope": np.asarray(L1_gnn_prelu_w).reshape(1, 1), "kept": kept, "setup": setup,
    }
    nc = bacc.Bacc("TRN2", target_bir_lowering=False, num_devices=1)
    args = [nc.dram_tensor("in_" + n, a.shape, mybir.dt.from_np(a.dtype), kind="ExternalInput").ap() for n, a in arrays.items()]
    args.append(nc.dram_tensor("out_0", (N, D), F32, kind="ExternalOutput").ap())
    for n, shape in (("rows", ((NB + 1) * P, 2 * R)), ("x1", (NW * BLK, D)), ("hs", (NW * BLK, D))):
        args.append(nc.dram_tensor(n + "_dram", shape, F32, kind="Internal").ap())
    gnn_kernel(nc, *args)
    r = run_bass_kernel_spmd(nc, [{"in_" + n: a for n, a in arrays.items()}], core_ids=[0])
    return r.results[0]["out_0"]
```

```python
import concourse.bass as bass
from concourse import mybir
import numpy as np
from contextlib import ExitStack

F32 = mybir.dt.float32
BF16 = mybir.dt.bfloat16
I32 = mybir.dt.int32
ALU = mybir.AluOpType
ACT = mybir.ActivationFunctionType
AX_X = mybir.AxisListType.X

N = 50000
E = 50000
D = 64
P = 128
BLK = 256
Q = 4
WIN = Q * P
NB = -(-E // BLK)
NW = -(-N // WIN)
HALF_BLOCKS = NB // 2
HALF = HALF_BLOCKS * BLK
COLS = 2 * BLK
CHUNKS = HALF_BLOCKS // 2
SETS = 2 * (-(-(NB + NW) // 8))
EARLY = CHUNKS + 1
STEPS = 4 * SETS
R = D + 1
PAD_NODE = NW * WIN - 1
TAIL_E = E - (NB - 1) * BLK
TAIL_N = N - (NW - 1) * WIN
NODES = NW * Q
BATCH = NODES // CHUNKS
WB = BATCH // Q
BIG = 1.0e38
EPS = 1e-5


def constants():
    p = np.arange(P)
    ident = np.eye(P)
    node_of = np.zeros((P, Q, P))
    node_of[:] = (Q * p[None, :] + np.arange(Q)[:, None])[None] - WIN // 2
    shift = np.zeros((P, P))
    shift[p[:64], p[:64] + 64] = 1.0
    kept = np.concatenate([ident, shift], 1)
    i = np.arange(HALF_BLOCKS)
    order = np.stack([4 * (i // 2) + i % 2, 4 * (i // 2) + 2 + i % 2])
    setup = np.zeros((P, STEPS + 4 * HALF_BLOCKS + 2 * NB + 2 + WIN))
    setup[:, :STEPS] = np.arange(STEPS)
    at = STEPS
    for h_from in range(2):
        for h_to in range(2):
            before = order[h_from][:, None] < order[h_to][None, :]
            setup[:HALF_BLOCKS, at:at + HALF_BLOCKS] = before
            at += HALF_BLOCKS
    for h in range(2):
        setup[i, at + order[h]] = 1.0
        at += NB
    for h in range(2):
        setup[:HALF_BLOCKS, at + h] = order[h]
    setup[:, at + 2:] = node_of.reshape(P, -1)
    return kept.astype(np.float32), setup.astype(np.float32)


def gnn_kernel(nc, x, src, dst, ef, ew, w0t, b0, w1t, b1, slope, kept_d, setup_d, out, rows_d, x1_d, hs_d):
    ctx = ExitStack()
    with ctx:
        def sb(name, shape, dt=F32):
            return ctx.enter_context(nc.sbuf_tensor(name, shape, dt))

        def sem(name):
            return ctx.enter_context(nc.semaphore(name))

        acc_t = sb("acc", [P, NODES * R])
        acc = acc_t[:, :].rearrange("p (w q r) -> p w q r", q=Q, r=R)
        accn = acc_t[:, :].rearrange("p (n r) -> p n r", r=R)
        kept = sb("kept", [P, 256])
        ident = kept[:, 0:128]
        shift = kept[:, 128:256]
        nident = sb("nident", [P, P])
        node_of16 = sb("node_of16", [P, WIN], BF16)
        minus_starts = sb("minus_starts", [P, COLS], BF16)
        spread = sb("spread", [2 * CHUNKS, CHUNKS, P], BF16)
        starts = sb("starts", [P, COLS], BF16)
        rel = sb("rel", [P, 2, STEPS])
        idx = sb("idx", [P, 2 * NB], I32)
        idx_h = sb("idx_h", [P, 2 * NB], I32)
        idx_now = [sb(f"idx_now{u}", [P, 8], I32) for u in range(4)]
        emit = sb("emit", [P, 2, 2, HALF_BLOCKS])
        ewe = sb("ewe", [P, 2, 2, HALF_BLOCKS])
        wtab = sb("wtab", [1, STEPS], I32)
        jtab = sb("jtab", [1, STEPS], I32)
        captab = sb("captab", [1, CHUNKS + 1], I32)
        w0 = sb("w0", [P, P])
        w1 = sb("w1", [P, P])
        b0r = sb("b0r", [P, R])
        b1r = sb("b1r", [P, D])
        slo = sb("slo", [P, 1])
        dinv = sb("dinv", [P, NODES])
        cap = sb("cap", [P, CHUNKS, 3])
        fixs = sb("fixs", [P, 16])
        fixf = sb("fixf", [1, D])
        fixrow = sb("fixrow", [P, 2, 3, R], BF16)
        onehot = sb("onehot", [P, 4, 2, WIN], BF16)
        steprow = sb("steprow", [P, 8, 2, 3, R], BF16)
        WORK = 13900
        work = sb("work", [P, WORK])

        class Carve:
            def __init__(self, t, end):
                self.t, self.at, self.end = t, 0, end

            def take(self, cols, parts=P):
                self.at += cols
                assert self.at <= self.end
                return self.t[0:parts, self.at - cols:self.at]

        HB = HALF_BLOCKS
        cs = Carve(acc_t, NODES * R)
        setc = cs.take(STEPS + 4 * HB + 2 * NB + 2 + WIN)
        kf = setc[:, 0:STEPS]
        before = setc[0:HB, STEPS:STEPS + 4 * HB].rearrange("p (a b i) -> p a b i", a=2, b=2)
        order = setc[0:HB, STEPS + 4 * HB + 2 * NB:STEPS + 4 * HB + 2 * NB + 2]
        node_of = setc[:, STEPS + 4 * HB + 2 * NB + 2:]
        nat = {}
        for nm in ("dst", "nxt", "src"):
            nat[nm + "i"] = cs.take(2 * BLK, HB).bitcast(I32)
            nat[nm] = cs.take(2 * BLK, HB)
        nat["ew"] = cs.take(2 * BLK, HB)
        dadj = cs.take(2 * BLK, HB)
        curi, prei = cs.take(COLS, 2 * CHUNKS).bitcast(I32), cs.take(COLS, 2 * CHUNKS).bitcast(I32)
        cur, pre = cs.take(COLS, 2 * CHUNKS), cs.take(COLS, 2 * CHUNKS)
        oh = cs.take(2 * STEPS, HB).rearrange("p (h k) -> p h k", h=2)
        oha = cs.take(2 * STEPS, HB).rearrange("p (h k) -> p h k", h=2)
        dste = cs.take(2 * NB).rearrange("p (t h i) -> p t h i", t=2, h=2)
        nxte = cs.take(2 * NB).rearrange("p (t h i) -> p t h i", t=2, h=2)
        crm = cs.take(2 * NB).rearrange("p (t h i) -> p t h i", t=2, h=2)
        fpi = cs.take(2, HB).bitcast(I32)
        fwi = cs.take(4, HB).bitcast(I32)
        fw = cs.take(4, HB)
        cnt = cs.take(2, HB)
        sst = cs.take(2, HB)
        sen = cs.take(2, HB)
        fms = cs.take(2, HB)
        fadj = cs.take(2, HB)
        crs = cs.take(1, HB)
        n0i = cs.take(1).bitcast(I32)
        n0 = cs.take(1)
        one = cs.take(1, HB)
        sc = cs.take(16, 1)
        sci = cs.take(4, 1).bitcast(I32)
        capf = cs.take(CHUNKS + 1, 1)
        rowf = cs.take(STEPS, 1)
        rowj = cs.take(STEPS, 1)
        idxf, quad_f, win_f = cs.take(2 * NB), cs.take(2 * NB), cs.take(2 * NB)
        quad, win = cs.take(2 * NB).bitcast(I32), cs.take(2 * NB).bitcast(I32)
        crj = cs.take(2 * BLK, HB)

        ca = Carve(work, WORK)
        g1 = [ca.take(8 * D) for _ in range(4)]
        m_s = [ca.take(COLS) for _ in range(2)]
        msa_w = [ca.take(3 * (COLS + 1)) for _ in range(2)]
        msa = [t.rearrange("p (a c) -> p a c", a=3) for t in msa_w]
        run_max, run_den, run_sum = [[t[:, a, :] for t in msa] for a in range(3)]
        ex = [ca.take(COLS) for _ in range(2)]
        dec = [ca.take(COLS) for _ in range(2)]
        mex = [ca.take(COLS) for _ in range(2)]
        rden = [ca.take(COLS) for _ in range(2)]
        q1 = [ca.take(COLS) for _ in range(2)]
        rows_w = [ca.take(8 * R) for _ in range(2)]
        rows = [t.rearrange("p (n r) -> p n r", r=R) for t in rows_w]
        parts_w = [ca.take(8 * 3 * R // 2).bitcast(BF16) for _ in range(2)]
        parts = [t.rearrange("p (n s r) -> p n s r", s=3, r=R) for t in parts_w]
        cb = Carve(work, WORK)
        xin = [cb.take(8 * D) for _ in range(4)]
        sq = [cb.take(8 * D) for _ in range(2)]
        x1s = [cb.take(8 * D) for _ in range(2)]
        xds = [cb.take(8 * D) for _ in range(2)]
        xdt = [cb.take(8 * D) for _ in range(2)]
        var, mean, rstd, rdin = [cb.take(NODES) for _ in range(4)]
        g3 = [cb.take(8 * D) for _ in range(4)]
        rows3_w = [cb.take(8 * R) for _ in range(2)]
        parts3_w = [cb.take(8 * 3 * R // 2).bitcast(BF16) for _ in range(2)]
        rows3 = [t.rearrange("p (n r) -> p n r", r=R) for t in rows3_w]
        parts3 = [t.rearrange("p (n s r) -> p n s r", s=3, r=R) for t in parts3_w]

        moved = work[:, 6160:6160 + 8 * Q * R].rearrange("p (k q r) -> p k q r", q=Q, r=R)

        bank = [ctx.enter_context(nc.psum_tensor(f"bank{i}", [P, 512], F32)) for i in range(8)]
        m_p, n_p, q_p = bank[0:2], bank[2], bank[3]
        h_p = bank[2:4]

        names = """passed pads nat_d nat_s nat_w flags_d misc_d consts_d weights_d dch src_ready ppe0 ppe1 ppe2 cst16 sources tables acc_init
        tr m_ready colmax max_ready z_ready relu_ready exp_ready sum_ready mex_ready den_ready rc_ln rc_ready q_ready w_ready
        captured fix_row fix_pe fix_q fix_a fix_store
        deg_max dinv_sqrt dinv_ready z1 z z_sum z_cen z_sq z_sum2 z_var z_std z_rstd z_rdin xd xd_t xd_tc hsp hs_acc x1m p3_clear
        o_sc o_b o_neg o_x o_z o_sum o_cen o_sq o_sum2 o_var o_std o_rstd o_out""".split()
        S = {n: sem("s_" + n) for n in names}
        ph = [{n: sem(f"s_{n}_{p}") for n in "rows_ready hi mid_in mid parts_ready built mm moved added".split()} for p in (1, 3)]
        for p, k in zip(ph, (1, 3)):
            p["stored"] = [sem(f"s_rows_stored{u}_{k}") for u in range(2)]
            p["steprow"] = [sem(f"s_steprow{u}_{k}") for u in range(8)]
        s_gath = [sem(f"s_gath{u}") for u in range(4)]
        s_idx = [sem(f"s_idx{u}") for u in range(4)]
        s_ef = [sem(f"s_ef{u}") for u in range(4)]
        s_xin = [sem(f"s_xin{u}") for u in range(4)]
        s_x1st = [sem(f"s_x1_stored{u}") for u in range(2)]
        s_hsst = [sem(f"s_hs_stored{u}") for u in range(2)]
        s_g3 = [sem(f"s_gath3_{u}") for u in range(4)]
        s_x1in = [sem(f"s_x1in{u}") for u in range(4)]
        s_outst = [sem(f"s_out_stored{u}") for u in range(2)]

        def held(eng):
            eng.sem_inc(S["passed"], 1)

        def first(c, ring=2):
            return isinstance(c, int) and c < ring

        def uses(u, ring=2):
            return -(-(CHUNKS - u) // ring)

        def staged(eng, *stages):
            stages = [(*st, CHUNKS)[:4] for st in stages]
            deep = max(lag for lag, _, _, _ in stages)
            head = (deep + 7) // 4

            def turn(c, r, i):
                for lag, f, ring, n in stages:
                    if not isinstance(c, int) or 0 <= c - lag < n:
                        u = (r - lag) % ring
                        f(c - lag, u, (4 // ring) * i + (r - lag - u) // ring)
            for c in range(4 * head):
                turn(c, c % 4, c // 4)
            with eng.Fori(head, CHUNKS // 4) as i:
                for r in range(4):
                    turn(4 * i + r if r else 4 * i, r, i)
            for c in range(CHUNKS // 4 * 4, max(lag + n for lag, _, _, n in stages)):
                turn(c, c % 4, c // 4)

        def at(ap, i, n=1):
            return ap[:, bass.ds(i, n)]

        def uslot(n, v, alone):
            return bank[4 * v + n if alone else 4 + n][:, 0:Q * R].rearrange("p (q r) -> p q r", q=Q)

        def add(eng, instr, p, k, ready, sums):
            eng.wait_ge(p[ready], k + 1 - (4 * EARLY if ready == "moved" else 0))
            w = eng.value_load(at(wtab[0:1, :], k), min_val=0, max_val=NW - 1)
            cols = R if p is ph[0] else D
            a = acc[:, bass.ds(w, 1), :, 0:cols].rearrange("p w q r -> p (w q) r")
            if not (isinstance(k, int) and k == 0):
                eng.wait_ge(p["added"], k)
            instr.tensor_tensor(a, a, sums[:, :, 0:cols], ALU.add).then_inc(p["added"], 1)


        def blocks_of(v, h, lo=0):
            base = h * HALF + lo
            full = HB if base + HB * BLK <= E else HB - 1
            main = v[base:base + full * BLK].rearrange("(i j) -> i j", j=BLK)
            rest = v[base + full * BLK:min(E, base + HB * BLK)] if full < HB else None
            return full, main, rest

        def win_view(a, b):
            return a[bass.ds(b * WB * WIN, WB * WIN), :].rearrange("(w p q) f -> p w (q f)", p=P, q=Q)

        def own_view(a, b):
            return a.rearrange("(p n) f -> p n f", p=P)[:, bass.ds(BATCH * b, BATCH), :]

        LAST = (CHUNKS - 1) * WB * WIN

        def full_windows(a):
            return a[LAST:LAST + (WB - 1) * WIN, :].rearrange("(w p q) f -> p w (q f)", p=P, q=Q)

        def short_window(a):
            return a[LAST + (WB - 1) * WIN:N, :].rearrange("(p q) f -> p (q f)", q=Q)

        block = ctx.enter_context(nc.Block())

        @block.sync
        def _(sp):
            sp.dma_start(kept[:, :], kept_d).then_inc(S["consts_d"], 16)
            sp.dma_start(setc, setup_d).then_inc(S["consts_d"], 16)
            sp.wait_ge(S["pads"], 1)
            for nm, v, lo, s in (("srci", src, 0, "nat_s"), ("dsti", dst, 0, "nat_d"), ("nxti", dst, 1, "nat_d"),
                                 ("ew", ew, 0, "nat_w")):
                for h in range(2):
                    full, main, rest = blocks_of(v, h, lo)
                    sp.dma_start(nat[nm][0:full, h * BLK:(h + 1) * BLK], main).then_inc(S[s], 16)
                    if rest is not None:
                        n = rest.shape[0]
                        sp.dma_start(nat[nm][full:full + 1, h * BLK:h * BLK + n],
                                     rest.rearrange("(a n) -> a n", a=1)).then_inc(S[s], 16)
            rows97 = 2 * CHUNKS - 1
            r = E - rows97 * COLS
            sp.dma_start(curi[0:rows97, :], dst[0:rows97 * COLS].rearrange("(a n) -> a n", n=COLS)).then_inc(S["flags_d"], 16)
            sp.dma_start(curi[rows97:rows97 + 1, 0:r],
                         dst[rows97 * COLS:E].rearrange("(a n) -> a n", a=1)).then_inc(S["flags_d"], 16)
            sp.dma_start(prei[0:1, 1:COLS], dst[0:COLS - 1].rearrange("(a n) -> a n", a=1)).then_inc(S["flags_d"], 16)
            sp.dma_start(prei[1:rows97, :],
                         dst[COLS - 1:rows97 * COLS - 1].rearrange("(a n) -> a n", n=COLS)).then_inc(S["flags_d"], 16)
            sp.dma_start(prei[rows97:rows97 + 1, 0:r],
                         dst[rows97 * COLS - 1:E - 1].rearrange("(a n) -> a n", a=1)).then_inc(S["flags_d"], 16)
            sp.dma_start(fpi[1:HB, 0:1], dst[BLK - 1:BLK - 1 + (HB - 1) * BLK].rearrange("(a n) -> a n", n=BLK)[:, 0:1], allow_slow_non_contiguous=True).then_inc(S["misc_d"], 16)
            sp.dma_start(fpi[0:HB, 1:2], dst.rearrange("(a n) -> a n", n=1)[HALF - 1:HALF + (HB - 1) * BLK:BLK, :], allow_slow_non_contiguous=True).then_inc(S["misc_d"], 16)
            sp.dma_start(n0i, dst[HALF - 1:HALF].rearrange("(a n) -> a n", a=1).broadcast_to([P, 1])).then_inc(S["misc_d"], 16)
            for t, d in ((w0, w0t), (w1, w1t)):
                for h in range(2):
                    sp.dma_start(t[h * D:(h + 1) * D, h * D:(h + 1) * D], d).then_inc(S["weights_d"], 16)
            sp.dma_start(b0r[:, 0:D], b0.rearrange("(a n) -> a n", a=1).broadcast_to([P, D])).then_inc(S["weights_d"], 16)
            sp.dma_start(b1r[:, :], b1.rearrange("(a n) -> a n", a=1).broadcast_to([P, D])).then_inc(S["weights_d"], 16)
            sp.dma_start(slo[:, :], slope.broadcast_to([P, 1])).then_inc(S["weights_d"], 16)

            def load_idx(c, u, table):
                sp.dma_start(idx_now[u][:, :], at(table[:, :], 8 * c, 8)).then_inc(s_idx[u], 16)

            def load_ef(c, u, i):
                if not first(c, 4):
                    sp.wait_ge(S["tr"], c - 3)
                for h in range(2):
                    d = g1[u].rearrange("p (n h f) -> p n h f", n=4, h=2)[:, :, h, :]
                    if isinstance(c, int) and c == CHUNKS - 1 and h == 1:
                        r0 = (NB - 2) * BLK
                        sp.dma_start(d[:, 0:2, :], ef[r0:r0 + BLK, :].rearrange("(n p) f -> p n f", p=P)).then_inc(s_ef[u], 16)
                        sp.dma_start(d[0:TAIL_E, 2:3, :].rearrange("p t f -> p (t f)"), ef[r0 + BLK:E, :]).then_inc(s_ef[u], 16)
                    else:
                        sp.dma_start(d, ef[bass.ds(c * COLS + h * HALF, COLS), :].rearrange("(n p) f -> p n f", p=P)).then_inc(s_ef[u], 16)
                if isinstance(c, int) and c == 0:
                    sp.wait_ge(S["sources"], 1)
                load_idx(c, u, idx)

            def store_rows(p, tiles):
                def f(c, u, i):
                    sp.wait_ge(p["parts_ready"], c + 1)
                    dview = rows_d[bass.ds(c * 4 * P, 4 * P), :].rearrange("(j p) f -> p j f", p=P)
                    sp.dma_start(dview, tiles[u].rearrange("p (j f) -> p j f", j=4)).then_inc(p["stored"][u], 16)
                return f

            def load_set(p):
                def f(s, v, i):
                    if not (isinstance(s, int) and s >= CHUNKS):
                        sp.wait_ge(p["stored"][v], 16 * (i + 1))
                        held(sp)
                    one_set(s, v, p)
                return f

            def one_set(s, v, p):
                for n in range(4):
                    k = 4 * s + n
                    if not first(s):
                        sp.wait_ge(p["mm"], k - 7)
                    if isinstance(k, int) and k == STEPS - 1:
                        sp.wait_ge(S["fix_store"], 16)
                        j = NB
                    else:
                        held(sp)
                        j = sp.value_load(at(jtab[0:1, :], k), min_val=0, max_val=NB - 1)
                    sp.dma_start(steprow[:, 4 * v + n, :, :, :].rearrange("p t s r -> p (t s r)"),
                                 rows_d[bass.ds(j * P, P), :]).then_inc(p["steprow"][4 * v + n], 16)

            def late_sets(p):
                with sp.Fori(EARLY // 2, SETS // 2 - 1) as i:
                    one_set(2 * i, 0, p)
                    one_set(2 * i + 1, 1, p)
                one_set(SETS - 2, 0, p)
                one_set(SETS - 1, 1, p)

            def wait_tables(c, u, i):
                if isinstance(c, int) and c == 0:
                    sp.wait_ge(S["tables"], 1)
            staged(sp, (5, store_rows(ph[0], parts_w), 2), (0, load_ef, 4), (6, wait_tables, 2), (6, load_set(ph[0]), 2, EARLY))
            sp.wait_ge(S["fix_row"], 1)
            sp.dma_start(rows_d[NB * P:(NB + 1) * P, :], fixrow[:, :, :, :].rearrange("p t s r -> p (t s r)")).then_inc(S["fix_store"], 16)
            late_sets(ph[0])

            def load_x(b, u, i):
                if not first(b, 4):
                    sp.wait_ge(S["z"], b - 3)
                tv = xin[u].rearrange("p (w f) -> p w f", w=WB)
                if isinstance(b, int) and b == CHUNKS - 1:
                    sp.dma_start(tv[:, 0:WB - 1, :], full_windows(x)).then_inc(s_xin[u], 16)
                    sp.dma_start(tv[0:TAIL_N // Q, WB - 1, :], short_window(x)).then_inc(s_xin[u], 16)
                else:
                    sp.dma_start(tv, win_view(x, b)).then_inc(s_xin[u], 16)

            def store2(b, u, i):
                sp.wait_ge(S["x1m"], b + 1)
                sp.dma_start(own_view(x1_d, b), x1s[u].rearrange("p (n f) -> p n f", f=D)).then_inc(s_x1st[u], 16)
                sp.wait_ge(S["hs_acc"], b + 1)
                sp.dma_start(own_view(hs_d, b), accn[:, bass.ds(BATCH * b, BATCH), 0:D]).then_inc(s_hsst[u], 16)

            sp.wait_ge(ph[0]["added"], STEPS)
            staged(sp, (7, store2, 2), (0, load_x, 4))

            def next_idx(c, u, i):
                if not first(c, 4):
                    sp.wait_ge(ph[1]["hi"], c - 3)
                load_idx(c, u, idx_h)
            staged(sp, (5, store_rows(ph[1], parts3_w), 2), (0, next_idx, 4), (6, load_set(ph[1]), 2, EARLY))
            late_sets(ph[1])

            for u in range(2):
                sp.wait_ge(s_x1st[u], 16 * uses(u))
            sp.wait_ge(ph[1]["added"], 4 * EARLY)

            def load_x1(b, u, i):
                if not first(b, 4):
                    sp.wait_ge(S["o_x"], b - 3)
                sp.dma_start(xin[u].rearrange("p (n f) -> p n f", f=D), own_view(x1_d, b)).then_inc(s_x1in[u], 16)

            def store_out(b, u, i):
                sp.wait_ge(S["o_out"], b + 1)
                tv = x1s[u].rearrange("p (w f) -> p w f", w=WB)
                if isinstance(b, int) and b == CHUNKS - 1:
                    sp.dma_start(full_windows(out), tv[:, 0:WB - 1, :]).then_inc(s_outst[u], 16)
                    sp.dma_start(short_window(out), tv[0:TAIL_N // Q, WB - 1, :]).then_inc(s_outst[u], 16)
                else:
                    sp.dma_start(win_view(out, b), tv).then_inc(s_outst[u], 16)
            staged(sp, (7, store_out, 2), (0, load_x1, 4))
            sp.wait_ge(s_outst[0], 16 * (uses(0) + 1))
            sp.wait_ge(s_outst[1], 16 * uses(1))

        @block.gpsimd
        def _(pool):
            def gather1(c, u, i):
                pool.wait_ge(s_idx[u], 16 * (i + 1))
                pool.wait_ge(s_ef[u], 32 * (i + 1) + (16 if isinstance(c, int) and c == CHUNKS - 1 else 0))
                held(pool)
                for h in range(2):
                    for b in range(2):
                        for t in range(2):
                            n, o = (2 * h + b) * 2 + t, ((2 * b + t) * 2 + h) * D
                            nc.gpsimd.indirect_dma_start(
                                g1[u][:, o:o + D], None, x[:, :],
                                bass.IndirectOffsetOnAxis(ap=idx_now[u][:, n:n + 1], axis=0),
                                compute_op=ALU.add).then_inc(s_gath[u], 16)
            staged(pool, (0, gather1, 4))

            def late_adds(p):
                with pool.Fori(EARLY // 2, SETS // 2) as i:
                    for v in range(2):
                        for n in range(4):
                            add(pool, nc.gpsimd, p, 8 * i + 4 * v + n, "moved", moved[:, 4 * v + n])
            late_adds(ph[0])

            def nodes(b):
                return accn[:, bass.ds(8 * b, 8), 0:D]

            def by_node(t, b):
                return t[:, bass.ds(8 * b, 8)].unsqueeze(2).broadcast_to([P, 8, D])

            def add_x(b, u, i):
                pool.wait_ge(S["z1"], b + 1)
                nc.gpsimd.tensor_tensor(nodes(b), nodes(b), xin[u].rearrange("p (n f) -> p n f", f=D), ALU.add).then_inc(S["z"], 1)

            def x1_mul(b, u, i):
                pool.wait_ge(S["z_rstd"], b + 1)
                if not first(b):
                    pool.wait_ge(s_x1st[u], 16 * i)
                nc.gpsimd.tensor_tensor(x1s[u].rearrange("p (n f) -> p n f", f=D), nodes(b), by_node(rstd, b), ALU.mult).then_inc(S["x1m"], 1)
            staged(pool, (0, add_x, 4), (3, x1_mul, 2))

            for u in range(2):
                pool.wait_ge(s_hsst[u], 16 * uses(u))

            def gather3(c, u, i):
                pool.wait_ge(s_idx[u], 16 * (uses(u, 4) + i + 1))
                held(pool)
                for n in range(8):
                    nc.gpsimd.indirect_dma_start(g3[u][:, n * D:(n + 1) * D], None, hs_d[:, :],
                        bass.IndirectOffsetOnAxis(ap=idx_now[u][:, n:n + 1], axis=0)).then_inc(s_g3[u], 16)
            staged(pool, (0, gather3, 4))
            late_adds(ph[1])

            def add_bias(b, u, i):
                pool.wait_ge(S["o_sc"], b + 1)
                nc.gpsimd.tensor_tensor(nodes(b), nodes(b), b1r[:, :].unsqueeze(1).broadcast_to([P, 8, D]), ALU.add).then_inc(S["o_b"], 1)

            def add_x1(b, u, i):
                pool.wait_ge(S["o_neg"], b + 1)
                pool.wait_ge(s_x1in[u], 16 * (i + 1))
                nc.gpsimd.tensor_tensor(xds[u % 2], xds[u % 2], xin[u], ALU.add).then_inc(S["o_x"], 1)

            def out_mul(b, u, i):
                pool.wait_ge(S["o_rstd"], b + 1)
                if not first(b):
                    pool.wait_ge(s_outst[u], 16 * i)
                nc.gpsimd.tensor_tensor(x1s[u].rearrange("p (n f) -> p n f", f=D), nodes(b), by_node(rstd, b), ALU.mult).then_inc(S["o_out"], 1)
            staged(pool, (0, add_bias, 2), (1, add_x1, 4), (5, out_mul, 2))

        @block.scalar
        def _(act):
            act.wait_ge(S["tables"], 1)
            act.wait_ge(S["weights_d"], 16 * 7)
            nc.scalar.activation(accn[:, :, :], b0r[:, :].unsqueeze(1).broadcast_to([P, NODES, R]), ACT.Copy).then_inc(S["acc_init"], 1)

            nc.scalar.preload_act_table_set("natural_log_exp_and_others")

            def copy_m(c, u, i):
                act.wait_ge(S["tr"], c + 1)
                if not first(c):
                    act.wait_ge(S["mex_ready"], c - 1)
                nc.scalar.activation(m_s[u], m_p[u][:, :], ACT.Copy).then_inc(S["m_ready"], 1)

            def recip(c, u, i):
                act.wait_ge(S["den_ready"], c + 1)
                if not first(c):
                    act.wait_ge(S["q_ready"], c - 1)
                nc.scalar.activation(rden[u], run_den[u][:, 1:], ACT.Ln).then_inc(S["rc_ln"], 1)
                act.wait_ge(S["rc_ln"], c + 1)
                nc.scalar.activation(rden[u], rden[u], ACT.Exp, scale=-1.0).then_inc(S["rc_ready"], 1)

            def exps(c, u, i):
                act.wait_ge(S["z_ready"], c + 1)
                if not first(c):
                    act.wait_ge(S["sum_ready"], c - 1)
                nc.scalar.activation(dec[u], m_p[u][:, :], ACT.Relu)
                nc.scalar.activation(ex[u], m_p[u][:, :], ACT.Relu, scale=-1.0).then_inc(S["relu_ready"], 1)
                act.wait_ge(S["relu_ready"], c + 1)
                nc.scalar.activation(dec[u], dec[u], ACT.Exp, scale=-1.0)
                nc.scalar.activation(ex[u], ex[u], ACT.Exp, scale=-1.0).then_inc(S["exp_ready"], 1)

            def high_part(p, r, t, u, c):
                act.wait_ge(p["rows_ready"], c + 1)
                nc.scalar.activation(t[u][:, :, 0, :], r[u][:, :, :], ACT.Copy).then_inc(p["hi"], 1)

            def middle_part(p, r, t):
                def f(c, u, i):
                    act.wait_ge(p["mid_in"], c + 1)
                    nc.scalar.activation(t[u][:, :, 1, :], r[u][:, :, :], ACT.Copy).then_inc(p["mid"], 1)
                return f

            def mask_rows(c, u, i):
                act.wait_ge(S["w_ready"], c + 1)
                if not first(c):
                    act.wait_ge(ph[0]["stored"][u], 16 * i)
                held(act)
                for h in range(2):
                    for b in range(2):
                        for t in range(2):
                            o = ((2 * b + t) * 2 + h) * D
                            nc.scalar.activation(rows[u][:, (2 * h + b) * 2 + t, 0:D], q_p[:, o:o + D], ACT.Copy,
                                                 scale=at(emit[:, t, h, :], 2 * c + b))
                    last = nc.scalar.activation(rows[u].rearrange("p (h b t) r -> p h b t r", h=2, b=2)[:, h, :, :, D],
                                                ewe[:, :, h, bass.ds(2 * c, 2)].rearrange("p t b -> p b t"), ACT.Copy)
                last.then_inc(ph[0]["rows_ready"], 1)
                high_part(ph[0], rows, parts, u, c)

            def capture(c, u, i):
                act.wait_ge(S["sum_ready"], c + 1)
                held(act)
                col = act.value_load(at(captab[0:1, :], c), min_val=0, max_val=COLS - 1)
                nc.scalar.activation(cap[:, bass.ds(c, 1), :].rearrange("p c a -> p a c"), msa[u][:, :, bass.ds(1 + col, 1)], ACT.Copy).then_inc(S["captured"], 1)

            staged(act, (0, copy_m, 2), (2, middle_part(ph[0], rows, parts), 2), (1, recip, 2), (0, exps, 2), (1, mask_rows, 2), (1, capture, 2))
            act.wait_ge(S["fix_q"], 1)
            nc.scalar.activation(fixs[:, 9:11], fixs[:, 7:9], ACT.Exp).then_inc(S["fix_a"], 1)

            def late_moves(p):
                act.wait_ge(p["added"], 4 * EARLY)
                cols = R if p is ph[0] else D
                with act.Fori(EARLY // 2, SETS // 2) as i:
                    for v in range(2):
                        for n in range(4):
                            k = 8 * i + 4 * v + n
                            act.wait_ge(p["mm"], k + 1)
                            act.wait_ge(p["added"], k - 7)
                            nc.scalar.activation(moved[:, 4 * v + n, :, 0:cols], uslot(n, v, True)[:, :, 0:cols], ACT.Copy).then_inc(p["moved"], 1)
            late_moves(ph[0])

            nc.scalar.preload_act_table_set("sqrt_and_others")
            act.wait_ge(S["deg_max"], 1)
            nc.scalar.activation(dinv[:, :], dinv[:, :], ACT.Sqrt).then_inc(S["dinv_sqrt"], 1)

            def square(cen, sum2, done):
                def f(b, u, i):
                    act.wait_ge(S[cen], b + 1)
                    if not first(b):
                        act.wait_ge(S[sum2], b - 1)
                    held(act)
                    nc.scalar.activation(sq[u].rearrange("p (n f) -> p n f", f=D), accn[:, bass.ds(8 * b, 8), 0:D], ACT.Square).then_inc(S[done], 1)
                return f

            def deviation(var_ready, done):
                def f(b, u, i):
                    act.wait_ge(S[var_ready], b + 1)
                    held(act)
                    nc.scalar.activation(at(rstd, 8 * b, 8), at(var, 8 * b, 8), ACT.Sqrt).then_inc(S[done], 1)
                return f

            def evac2(b, u, i):
                act.wait_ge(S["xd_t"], b + 1)
                if not first(b):
                    act.wait_ge(S["hsp"], b - 1)
                nc.scalar.activation(xdt[u], m_p[u][:, :], ACT.Copy).then_inc(S["xd_tc"], 1)

            def keep_h(b, u, i):
                act.wait_ge(S["hsp"], b + 1)
                act.wait_ge(S["x1m"], b + 1)
                act.wait_ge(S["xd"], b + 1)
                held(act)
                nc.scalar.activation(accn[:, bass.ds(8 * b, 8), 0:D], h_p[u][:, :].rearrange("p (n f) -> p n f", f=D), ACT.Copy).then_inc(S["hs_acc"], 1)
            staged(act, (1, square("z_cen", "z_sum2", "z_sq"), 2), (4, evac2, 2), (2, deviation("z_var", "z_std"), 2), (5, keep_h, 2))

            def weight_rows(c, u, i):
                act.wait_ge(s_g3[u], 128 * (i + 1))
                v, before = u % 2, 2 * i + u // 2
                if not first(c):
                    act.wait_ge(ph[1]["stored"][v], 16 * before)
                held(act)
                for h in range(2):
                    for b in range(2):
                        for t in range(2):
                            n = (2 * h + b) * 2 + t
                            last = nc.scalar.activation(rows3[v][:, n, 0:D], g3[u][:, n * D:(n + 1) * D], ACT.Copy,
                                                        scale=at(ewe[:, t, h, :], 2 * c + b))
                last.then_inc(ph[1]["rows_ready"], 1)
                high_part(ph[1], rows3, parts3, v, c)
            act.wait_ge(S["p3_clear"], 1)
            staged(act, (2, middle_part(ph[1], rows3, parts3), 2), (1, weight_rows, 4))
            late_moves(ph[1])

            staged(act, (2, square("o_cen", "o_sum2", "o_sq"), 2), (3, deviation("o_var", "o_std"), 2))

        @block.vector
        def _(dve):
            chain = [0]

            def link(ins):
                chain[0] += 1
                ins.then_inc(S["dch"], 1)
                dve.wait_ge(S["dch"], chain[0])

            V = nc.vector
            V.memset(nat["srci"], 0)
            V.memset(nat["dsti"], PAD_NODE)
            V.memset(nat["nxti"], PAD_NODE + 1)
            V.memset(nat["ew"], 0.0)
            V.memset(curi, PAD_NODE)
            V.memset(prei, -1)
            V.memset(fpi, 0)
            V.memset(w0[:, :], 0.0)
            V.memset(w1[:, :], 0.0)
            V.memset(b0r[:, :], 1.0)
            V.memset(one, 1.0)
            V.memset(fixrow[:, :, :, :], 0.0)
            V.memset(run_max[1][:, COLS:], -BIG)
            V.memset(run_den[1][:, COLS:], 0.0)
            V.memset(run_sum[1][:, COLS:], 0.0).then_inc(S["pads"], 1)
            dve.wait_ge(S["consts_d"], 32)
            V.tensor_copy(node_of16[:, :], node_of)
            dve.wait_ge(S["nat_s"], 16 * 3)
            V.tensor_copy(nat["src"], nat["srci"]).then_inc(S["src_ready"], 1)
            dve.wait_ge(S["ppe0"], 1)
            for t in range(2):
                for h in range(2):
                    V.tensor_copy(idx[:, :].rearrange("p (c h b t) -> p h t c b", h=2, b=2, t=2)[:, h, t, :, :],
                                  bank[2][:, (2 * t + h) * HB:(2 * t + h + 1) * HB].rearrange("p (c b) -> p c b", b=2))
            V.memset(sc[:, 14:15], 0.0).then_inc(S["sources"], 1)
            dve.wait_ge(S["nat_d"], 16 * 6)
            dve.wait_ge(S["nat_w"], 16 * 3)
            dve.wait_ge(S["flags_d"], 16 * 5)
            dve.wait_ge(S["misc_d"], 16 * 3)
            for nm in ("dst", "nxt"):
                V.tensor_copy(nat[nm], nat[nm + "i"])
            V.tensor_copy(cur, curi)
            V.tensor_copy(pre, prei)
            V.tensor_copy(n0, n0i)
            for h in range(2):
                V.tensor_copy(spread[:, :, h * D:(h + 1) * D],
                              ident[0:2 * CHUNKS, h * CHUNKS:(h + 1) * CHUNKS].unsqueeze(2).broadcast_to([2 * CHUNKS, CHUNKS, D]))
            V.tensor_scalar(nident[:, :], ident, -1.0, None, ALU.mult)
            V.tensor_copy(fwi[:, 0:2], fpi)
            link(V.tensor_copy(fwi[:, 2:4], nat["dsti"].rearrange("p (h j) -> p h j", h=2)[:, :, BLK - 1]))
            link(V.tensor_single_scalar(fwi, fwi, 9, ALU.arith_shift_right))
            link(V.tensor_copy(fw, fwi))
            link(V.tensor_tensor(cnt, fw[:, 2:4], fw[:, 0:2], ALU.subtract))
            link(V.tensor_scalar(cnt, cnt, 1.0, None, ALU.add))
            link(V.tensor_scalar(crj[:, 0:BLK], nat["dst"][:, BLK:2 * BLK], n0[0:HB, :], 0.0, ALU.is_equal, ALU.add, accum_out=crs))
            link(V.tensor_tensor(cur, cur, pre, ALU.is_equal))
            V.tensor_scalar(minus_starts[0:2 * CHUNKS, :], cur, -1.0, -BIG, ALU.add, ALU.mult)
            V.tensor_scalar(starts[0:2 * CHUNKS, :], cur, -1.0, BIG, ALU.add, ALU.mult).then_inc(S["cst16"], 1)
            dve.wait_ge(S["ppe1"], 1)
            V.tensor_copy(dste.rearrange("p t h i -> p (t h i)"), bank[0][:, 0:2 * NB])
            V.tensor_copy(nxte.rearrange("p t h i -> p (t h i)"), bank[1][:, 0:2 * NB])
            V.tensor_copy(ewe[:, :, :, :].rearrange("p t h i -> p (t h i)"), bank[3][:, 0:2 * NB])
            V.tensor_copy(sst, bank[4][0:HB, 0:2])
            link(V.tensor_copy(sc[:, 0:1], bank[5][0:1, 0:1]))
            V.tensor_tensor(emit[:, :, :, :].rearrange("p t h i -> p (t h i)"), dste.rearrange("p t h i -> p (t h i)"),
                            nxte.rearrange("p t h i -> p (t h i)"), ALU.not_equal)
            link(V.tensor_scalar(crm[:, :, 1, :], dste[:, :, 1, :], n0, None, ALU.not_equal))
            link(V.tensor_tensor(emit[:, :, 1, :], emit[:, :, 1, :], crm[:, :, 1, :], ALU.mult))
            V.tensor_tensor(fms, fw[:, 0:2], sst, ALU.subtract)
            link(V.tensor_tensor(sen, sst, cnt, ALU.add))
            link(V.tensor_scalar(fadj, fms, -float(WIN), -float(WIN // 2), ALU.mult, ALU.add))
            for h in range(2):
                V.tensor_scalar(oha[:, h, :], kf[0:HB, :], sst[:, h:h + 1], None, ALU.is_ge)
                V.tensor_scalar(dadj[:, h * BLK:(h + 1) * BLK], nat["dst"][:, h * BLK:(h + 1) * BLK], fadj[:, h:h + 1], None, ALU.add)
            link(V.tensor_copy(sc[:, 1:2], n0[0:1, :]))
            for h in range(2):
                last = V.scalar_tensor_tensor(oh[:, h, :], kf[0:HB, :], sen[:, h:h + 1], oha[:, h, :], ALU.is_lt, ALU.mult)
            link(last)
            V.tensor_copy(sci[:, 0:1], n0i[0:1, :]).then_inc(S["cst16"], 1)
            dve.wait_ge(S["cst16"], 2)
            link(V.tensor_single_scalar(sci[:, 0:1], sci[:, 0:1], 9, ALU.arith_shift_right))
            V.tensor_copy(sc[:, 4:5], sci[:, 0:1])
            V.tensor_scalar(sc[:, 2:3], sc[:, 0:1], 1.0, None, ALU.is_ge)
            link(V.tensor_scalar(sc[:, 3:4], sc[:, 0:1], -1.0, 0.0, ALU.add, ALU.max))
            link(V.tensor_scalar(sc[:, 6:7], sc[:, 4:5], -float(WIN), 1.0, ALU.mult, ALU.add))
            link(V.tensor_tensor(sc[:, 5:6], sc[:, 6:7], sc[:, 1:2], ALU.add))
            link(V.tensor_tensor(sc[:, 5:6], sc[:, 5:6], sc[:, 2:3], ALU.mult))
            link(V.tensor_scalar(capf, kf[0:1, 0:CHUNKS + 1], -float(COLS), sc[:, 3:4], ALU.mult, ALU.add))
            link(V.tensor_scalar(capf, capf, 0.0, float(COLS - 1), ALU.max, ALU.min))
            V.tensor_copy(captab[:, :], capf)
            link(V.tensor_copy(sci[:, 1:2], sc[:, 3:4]))
            link(V.tensor_single_scalar(sci[:, 1:2], sci[:, 1:2], 9, ALU.arith_shift_right))
            V.tensor_copy(captab[:, CHUNKS:CHUNKS + 1], sci[:, 1:2])
            dve.wait_ge(S["ppe2"], 1)
            for t in range(2):
                V.scalar_tensor_tensor(rel[:, t, :], kf, -float(WIN), bank[t][:, 0:STEPS], ALU.mult, ALU.add)
            V.tensor_tensor(rowf, bank[4][0:1, 0:STEPS], kf[0:1, :], ALU.add)
            V.tensor_copy(rowj, bank[5][0:1, 0:STEPS])
            link(V.tensor_scalar(sc[:, 7:8], sc[:, 5:6], -1.0 - WIN // 2, None, ALU.add))
            V.tensor_copy(rel[0:1, 0, STEPS - 1:], sc[:, 7:8])
            V.tensor_copy(rowf[:, STEPS - 1:], sc[:, 4:5])
            link(V.memset(rowj[:, STEPS - 1:], float(NB - 1)))
            link(V.tensor_scalar(rowf, rowf, float(NW - 1), None, ALU.min))
            V.tensor_copy(wtab[:, :], rowf)
            V.tensor_copy(jtab[:, :], rowj)
            V.tensor_single_scalar(quad, idx[:, :], 2, ALU.arith_shift_right)
            V.tensor_single_scalar(win, idx[:, :], 9, ALU.arith_shift_right)
            link(V.tensor_copy(idxf, idx[:, :]))
            V.tensor_copy(quad_f, quad)
            link(V.tensor_copy(win_f, win))
            link(V.scalar_tensor_tensor(idxf, quad_f, float(NODES - Q), idxf, ALU.mult, ALU.add))
            link(V.scalar_tensor_tensor(idxf, win_f, float(Q - P * NODES), idxf, ALU.mult, ALU.add))
            link(V.tensor_copy(idx_h[:, :], idxf))
            V.memset(sc[:, 15:16], 0.0).then_inc(S["tables"], 1)

            def build_set(p):
                def f(s, v, i):
                    if not (isinstance(s, int) and s == 0):
                        dve.wait_ge(p["mm"], 4 * s)
                    for n in range(4):
                        for t in range(2):
                            last = V.tensor_scalar(onehot[:, n, t, :], node_of16[:, :], at(rel[:, t, :], 4 * s + n), None, ALU.is_equal)
                        last.then_inc(p["built"], 1)
                return f

            def add_set(p):
                def f(s, v, i):
                    if p is ph[0] and isinstance(s, int) and s == 0:
                        dve.wait_ge(S["acc_init"], 1)
                    for n in range(4):
                        add(dve, V, p, 4 * s + n, "mm", uslot(n, v, False))
                return f

            def late_sets(p):
                with dve.Fori(EARLY, SETS) as s:
                    for n in range(4):
                        dve.wait_ge(p["mm"], 4 * s + n - 3)
                        for t in range(2):
                            last = V.tensor_scalar(onehot[:, n, t, :], node_of16[:, :], at(rel[:, t, :], 4 * s + n), None, ALU.is_equal)
                        last.then_inc(p["built"], 1)

            def after_high(p, r, t):
                def f(c, u, i):
                    dve.wait_ge(p["hi"], c + 1)
                    V.tensor_tensor(r[u][:, :, :], r[u][:, :, :], t[u][:, :, 0, :], ALU.subtract).then_inc(p["mid_in"], 1)
                return f

            def low_part(p, r, t):
                def f(c, u, i):
                    dve.wait_ge(p["mid"], c + 1)
                    V.tensor_tensor(t[u][:, :, 2, :], r[u][:, :, :], t[u][:, :, 1, :], ALU.subtract).then_inc(p["parts_ready"], 1)
                return f

            def scan_max(c, u, i):
                dve.wait_ge(S["m_ready"], c + 1)
                if not (isinstance(c, int) and c == 0):
                    dve.wait_ge(S["max_ready"], c)
                if not first(c):
                    dve.wait_ge(S["z_ready"], c - 1)
                    dve.wait_ge(S["captured"], c - 1)
                V.tensor_copy(run_max[u][:, 0:1], run_max[1 - u][:, COLS:]).then_inc(S["colmax"], 1)
                dve.wait_ge(S["colmax"], c + 1)
                V.tensor_tensor_scan(run_max[u][:, 1:], n_p[:, :], m_s[u], run_max[u][:, 0:1], ALU.add, ALU.max).then_inc(S["max_ready"], 1)

            def scan_sums(c, u, i):
                dve.wait_ge(S["exp_ready"], c + 1)
                if not first(c):
                    dve.wait_ge(S["rc_ready"], c - 1)
                if not (isinstance(c, int) and c == 0):
                    dve.wait_ge(S["sum_ready"], c)
                V.tensor_tensor_scan(run_den[u][:, 1:], dec[u], ex[u], run_den[1 - u][:, COLS:], ALU.mult, ALU.add).then_inc(S["den_ready"], 1)
                V.tensor_tensor(mex[u], m_s[u], ex[u], ALU.mult).then_inc(S["mex_ready"], 1)
                dve.wait_ge(S["mex_ready"], c + 1)
                V.tensor_tensor_scan(run_sum[u][:, 1:], dec[u], mex[u], run_sum[1 - u][:, COLS:], ALU.mult, ALU.add).then_inc(S["sum_ready"], 1)

            def quotient(c, u, i):
                dve.wait_ge(S["rc_ready"], c + 1)
                dve.wait_ge(S["sum_ready"], c + 1)
                if not first(c):
                    dve.wait_ge(S["w_ready"], c - 1)
                V.scalar_tensor_tensor(q1[u], rden[u], 1.0e38, run_sum[u][:, 1:], ALU.min, ALU.mult).then_inc(S["q_ready"], 1)

            staged(dve, (0, scan_max, 2), (6, add_set(ph[0]), 2, EARLY), (5, build_set(ph[0]), 2, EARLY), (2, low_part(ph[0], rows, parts), 2),
                   (1, quotient, 2), (0, scan_sums, 2), (1, after_high(ph[0], rows, parts), 2))

            def fix_crossing():
                dve.wait_ge(S["captured"], CHUNKS)
                cc = dve.value_load(captab[0:1, CHUNKS:CHUNKS + 1], min_val=0, max_val=CHUNKS - 1)
                V.tensor_copy(fixs[:, 3:6], cap[:, bass.ds(cc, 1), :].rearrange("p c a -> p (c a)"))
                dve.wait_ge(S["fix_pe"], 1)
                link(V.tensor_copy(fixs[:, 0:3], bank[7][:, 400:403]))
                link(V.tensor_tensor(fixs[:, 6:7], fixs[:, 0:1], fixs[:, 3:4], ALU.max))
                V.tensor_tensor(fixs[:, 7:8], fixs[:, 0:1], fixs[:, 6:7], ALU.subtract)
                V.tensor_tensor(fixs[:, 8:9], fixs[:, 3:4], fixs[:, 6:7], ALU.subtract).then_inc(S["fix_q"], 1)
                dve.wait_ge(S["fix_a"], 1)
                V.tensor_scalar(fixs[:, 1:3], fixs[:, 1:3], fixs[:, 9:10], None, ALU.mult)
                link(V.tensor_scalar(fixs[:, 4:6], fixs[:, 4:6], fixs[:, 10:11], None, ALU.mult))
                link(V.tensor_tensor(fixs[:, 1:3], fixs[:, 1:3], fixs[:, 4:6], ALU.add))
                link(V.tensor_scalar(fixs[:, 1:2], fixs[:, 1:2], 1.0e-38, None, ALU.max))
                link(V.reciprocal(fixs[:, 1:2], fixs[:, 1:2]))
                V.tensor_tensor(fixs[:, 11:12], fixs[:, 1:2], fixs[:, 2:3], ALU.mult).then_inc(S["fix_q"], 1)
                dve.wait_ge(S["fix_pe"], 2)
                link(V.tensor_copy(fixf[:, :], bank[7][0:1, D:2 * D]))
                for part in range(2):
                    link(V.tensor_copy(fixrow[0:1, 0, part, 0:D], fixf[:, :]))
                    link(V.tensor_tensor(fixf[:, :], fixf[:, :], fixrow[0:1, 0, part, 0:D], ALU.subtract))
                V.tensor_copy(fixrow[0:1, 0, 2, 0:D], fixf[:, :]).then_inc(S["fix_row"], 1)
            fix_crossing()
            late_sets(ph[0])

            dve.wait_ge(ph[0]["added"], STEPS)
            V.tensor_scalar(dinv[:, :], accn[:, :, D], 1.0e-12, None, ALU.max).then_inc(S["deg_max"], 1)
            V.tensor_scalar(rdin, accn[:, :, D], 0.0, None, ALU.is_gt)
            dve.wait_ge(S["dinv_sqrt"], 1)
            link(V.reciprocal(dinv[:, :], dinv[:, :]))
            link(V.tensor_tensor(dinv[:, :], dinv[:, :], rdin, ALU.mult))

            def nodes(b):
                return accn[:, bass.ds(8 * b, 8), 0:D]

            def by_node(t, b):
                return t[:, bass.ds(8 * b, 8)].unsqueeze(2).broadcast_to([P, 8, D])

            def relu_x(b, u, i):
                dve.wait_ge(s_xin[u], 16 * (i + 1) + (16 if isinstance(b, int) and b == CHUNKS - 1 else 0))
                V.scalar_tensor_tensor(nodes(b), nodes(b), 0.0, xin[u].rearrange("p (n f) -> p n f", f=D), ALU.max, ALU.add).then_inc(S["z1"], 1)

            def centre(ready, summed, done):
                def f(b, u, i):
                    dve.wait_ge(S[ready], b + 1)
                    V.reduce_sum(at(mean, 8 * b, 8), nodes(b), AX_X).then_inc(S[summed], 1)
                    dve.wait_ge(S[summed], b + 1)
                    V.scalar_tensor_tensor(nodes(b), by_node(mean, b), -1.0 / D, nodes(b), ALU.mult, ALU.add).then_inc(S[done], 1)
                return f

            def variance(ready, summed, done):
                def f(b, u, i):
                    dve.wait_ge(S[ready], b + 1)
                    V.reduce_sum(at(var, 8 * b, 8), sq[u].rearrange("p (n f) -> p n f", f=D), AX_X).then_inc(S[summed], 1)
                    dve.wait_ge(S[summed], b + 1)
                    V.tensor_scalar(at(var, 8 * b, 8), at(var, 8 * b, 8), 1.0 / D, EPS, ALU.mult, ALU.add).then_inc(S[done], 1)
                return f

            def inverse(ready, done):
                def f(b, u, i):
                    dve.wait_ge(S[ready], b + 1)
                    V.reciprocal(at(rstd, 8 * b, 8), at(rstd, 8 * b, 8)).then_inc(S[done], 1)
                return f

            def scale_d(b, u, i):
                dve.wait_ge(S["z_rstd"], b + 1)
                V.tensor_tensor(at(rdin, 8 * b, 8), at(rstd, 8 * b, 8), at(dinv[:, :], 8 * b, 8), ALU.mult).then_inc(S["z_rdin"], 1)
                dve.wait_ge(S["z_rdin"], b + 1)
                if not first(b):
                    dve.wait_ge(S["xd_t"], b - 1)
                V.tensor_tensor(xds[u].rearrange("p (n f) -> p n f", f=D), nodes(b), by_node(rdin, b), ALU.mult).then_inc(S["xd"], 1)
            staged(dve, (0, relu_x, 4), (2, variance("z_sq", "z_sum2", "z_var"), 2), (1, centre("z", "z_sum", "z_cen"), 2),
                   (3, inverse("z_std", "z_rstd"), 2), (3, scale_d, 2))

            dve.wait_ge(S["hs_acc"], CHUNKS)
            for t in rows3:
                V.memset(t[:, :, D:], 0.0)
            V.memset(rel[0:1, 0, STEPS - 1:], float(WIN)).then_inc(S["p3_clear"], 1)
            for u in range(2):
                dve.wait_ge(s_hsst[u], 16 * uses(u))
            staged(dve, (6, add_set(ph[1]), 2, EARLY), (5, build_set(ph[1]), 2, EARLY), (2, low_part(ph[1], rows3, parts3), 2),
                   (1, after_high(ph[1], rows3, parts3), 2))
            late_sets(ph[1])

            dve.wait_ge(ph[1]["added"], STEPS)

            def scale_sum(b, u, i):
                V.tensor_tensor(nodes(b), nodes(b), by_node(dinv, b), ALU.mult).then_inc(S["o_sc"], 1)

            def negatives(b, u, i):
                dve.wait_ge(S["o_b"], b + 1)
                if not first(b):
                    dve.wait_ge(S["o_z"], b - 1)
                V.tensor_scalar(xds[u].rearrange("p (n f) -> p n f", f=D), nodes(b), 0.0, slo[:, 0:1], ALU.min, ALU.mult).then_inc(S["o_neg"], 1)

            def residual(b, u, i):
                dve.wait_ge(S["o_x"], b + 1)
                V.scalar_tensor_tensor(nodes(b), nodes(b), 0.0, xds[u].rearrange("p (n f) -> p n f", f=D), ALU.max, ALU.add).then_inc(S["o_z"], 1)

            staged(dve, (0, scale_sum, 2), (3, variance("o_sq", "o_sum2", "o_var"), 2), (1, negatives, 2), (2, residual, 2),
                   (2, centre("o_z", "o_sum", "o_cen"), 2), (4, inverse("o_std", "o_rstd"), 2))

        @block.tensor
        def _(pe):
            T = nc.tensor
            pe.wait_ge(S["src_ready"], 1)
            for bk, nm in ((2, "src"), (0, "dst"), (1, "nxt"), (3, "ew")):
                if nm == "dst":
                    last.then_inc(S["ppe0"], 1)
                    pe.wait_ge(S["cst16"], 1)
                for t in range(2):
                    for h in range(2):
                        o = (t * 2 + h) * HB
                        last = T.matmul(bank[bk][:, o:o + HB], nat[nm][:, h * BLK + t * P:h * BLK + (t + 1) * P], ident[0:HB, 0:HB],
                                 start=True, stop=True)
            for h in range(2):
                for hf in range(2):
                    T.matmul(bank[4][0:HB, h:h + 1], before[:, hf, h, :], cnt[:, hf:hf + 1], start=(hf == 0), stop=(hf == 1))
            T.matmul(bank[5][0:1, 0:1], crs, one, start=True, stop=True).then_inc(S["ppe1"], 1)
            pe.wait_ge(S["cst16"], 2)
            for t in range(2):
                for h in range(2):
                    T.matmul(bank[t][:, 0:STEPS], dadj[:, h * BLK + t * P:h * BLK + (t + 1) * P], oh[:, h, :], start=(h == 0), stop=(h == 1))
            for h in range(2):
                T.matmul(bank[4][0:1, 0:STEPS], fms[:, h:h + 1], oh[:, h, :], start=(h == 0), stop=(h == 1))
            for h in range(2):
                last = T.matmul(bank[5][0:1, 0:STEPS], order[:, h:h + 1], oh[:, h, :], start=(h == 0), stop=(h == 1))
            last.then_inc(S["ppe2"], 1)

            def steps(p, s, v, i, alone):
                for n in range(4):
                    k = 4 * s + n
                    pe.wait_ge(p["steprow"][4 * v + n], 16 * (i + 1))
                    pe.wait_ge(p["built"], k + 1)
                    if alone and not (isinstance(s, int) and s < EARLY + 2):
                        pe.wait_ge(p["moved"], k - 7 - 4 * EARLY)
                    elif alone:
                        pe.wait_ge(p["added"], 4 * EARLY)
                    elif not (isinstance(s, int) and s == 0):
                        pe.wait_ge(p["added"], 4 * s)
                    u = uslot(n, v, alone)
                    cols = R if p is ph[0] else D
                    for q in range(Q):
                        for t in range(2):
                            for part in range(3):
                                last = T.matmul(u[:, q, 0:cols], onehot[:, n, t, q * P:(q + 1) * P], steprow[:, 4 * v + n, t, part, 0:cols],
                                                start=(t == 0 and part == 0), stop=(t == 1 and part == 2))
                    last.then_inc(p["mm"], 1)

            def early_sets(p):
                return lambda s, v, i: steps(p, s, v, i, False)

            def late_sets(p):
                pe.wait_ge(p["added"], 4 * EARLY)
                for v in range(2):
                    steps(p, EARLY + v, v, EARLY // 2, True)
                with pe.Fori(EARLY // 2 + 1, SETS // 2) as i:
                    steps(p, 2 * i, 0, i, True)
                    steps(p, 2 * i + 1, 1, i, True)

            def transposes(c, u4, i):
                pe.wait_ge(s_gath[u4], 128 * (i + 1))
                u = u4 % 2
                if not first(c):
                    pe.wait_ge(S["exp_ready"], c - 1)
                if not first(c, 1):
                    pe.wait_ge(S["max_ready"], c)
                sel = spread[:, bass.ds(c, 1), :].rearrange("k c m -> k (c m)")
                T.matmul(n_p[:, :], sel, starts[0:2 * CHUNKS, :], start=True, stop=True)
                for n in range(4):
                    last = T.matmul(m_p[u][:, n * P:(n + 1) * P], g1[u4][:, n * P:(n + 1) * P], ident, start=(n == 0), stop=(n == 3),
                                    is_transpose=True, skip_group_check=True)
                last.then_inc(S["tr"], 1)

            def against_max(c, u, i):
                pe.wait_ge(S["max_ready"], c + 1)
                sel = spread[:, bass.ds(c, 1), :].rearrange("k c m -> k (c m)")
                T.matmul(m_p[u][:, :], sel, minus_starts[0:2 * CHUNKS, :], start=False, stop=False, skip_group_check=True)
                T.matmul(m_p[u][:, :], nident[:, :], run_max[u][:, 0:COLS], start=False, stop=True, skip_group_check=True).then_inc(S["z_ready"], 1)

            def product(c, u, i):
                pe.wait_ge(S["q_ready"], c + 1)
                if not first(c, 1):
                    pe.wait_ge(ph[0]["rows_ready"], c)
                for b in range(2):
                    for t in range(2):
                        o = (2 * b + t) * P
                        last = T.matmul(q_p[:, o:o + P], q1[u][:, o:o + P], w0[:, :], start=True, stop=True)
                last.then_inc(S["w_ready"], 1)

            pe.wait_ge(S["sources"], 1)
            pe.wait_ge(S["tables"], 1)
            pe.wait_ge(S["weights_d"], 16 * 7)
            staged(pe, (0, transposes, 4), (0, against_max, 2), (1, product, 2), (5, early_sets(ph[0]), 2, EARLY))
            pe.wait_ge(ph[0]["added"], 4 * EARLY)
            pe.wait_ge(S["sum_ready"], CHUNKS)
            T.matmul(bank[7][:, 400:403], shift, msa[0][:, :, COLS], start=True, stop=True).then_inc(S["fix_pe"], 1)
            pe.wait_ge(S["fix_q"], 2)
            T.matmul(bank[7][0:1, 0:P], fixs[:, 11:12], w0[:, :], start=True, stop=True).then_inc(S["fix_pe"], 1)
            pe.wait_ge(S["fix_row"], 1)
            late_sets(ph[0])

            pe.wait_ge(ph[0]["added"], STEPS)

            def transpose2(b, u, i):
                pe.wait_ge(S["xd"], b + 1)
                if not first(b):
                    pe.wait_ge(S["xd_tc"], b - 1)
                for w in range(4):
                    last = T.matmul(m_p[u][:, w * P:(w + 1) * P], xds[u][:, w * P:(w + 1) * P], ident, start=True, stop=True, is_transpose=True)
                last.then_inc(S["xd_t"], 1)

            def product2(b, u, i):
                pe.wait_ge(S["xd_tc"], b + 1)
                if not first(b):
                    pe.wait_ge(S["hs_acc"], b - 1)
                for w in range(4):
                    last = T.matmul(h_p[u][:, w * P:(w + 1) * P], xdt[u][:, w * P:(w + 1) * P], w1[:, :], start=True, stop=True)
                last.then_inc(S["hsp"], 1)
            staged(pe, (3, transpose2, 2), (4, product2, 2))

            pe.wait_ge(S["hs_acc"], CHUNKS)
            staged(pe, (5, early_sets(ph[1]), 2, EARLY))
            late_sets(ph[1])


def kernel(x, src, dst, edge_attr_64, edge_weight, L0_gnn_W, L0_gnn_b, L1_gnn_W, L1_gnn_bias, L1_gnn_prelu_w):
    import concourse.bacc as bacc
    from concourse.bass_utils import run_bass_kernel_spmd

    kept, setup = constants()
    arrays = {
        "x": np.asarray(x), "src": np.asarray(src), "dst": np.asarray(dst),
        "ef": np.asarray(edge_attr_64), "ew": np.asarray(edge_weight),
        "w0t": np.ascontiguousarray(np.asarray(L0_gnn_W).T), "b0": np.asarray(L0_gnn_b),
        "w1t": np.ascontiguousarray(np.asarray(L1_gnn_W).T), "b1": np.asarray(L1_gnn_bias),
        "slope": np.asarray(L1_gnn_prelu_w).reshape(1, 1), "kept": kept, "setup": setup,
    }
    nc = bacc.Bacc("TRN2", target_bir_lowering=False, num_devices=1)
    args = [nc.dram_tensor("in_" + n, a.shape, mybir.dt.from_np(a.dtype), kind="ExternalInput").ap() for n, a in arrays.items()]
    args.append(nc.dram_tensor("out_0", (N, D), F32, kind="ExternalOutput").ap())
    for n, shape in (("rows", ((NB + 1) * P, 2 * 3 * R)), ("x1", (P * NODES, D)), ("hs", (P * NODES, D))):
        args.append(nc.dram_tensor(n + "_dram", shape, BF16 if n == "rows" else F32, kind="Internal").ap())
    gnn_kernel(nc, *args)
    r = run_bass_kernel_spmd(nc, [{"in_" + n: a for n, a in arrays.items()}], core_ids=[0])
    return r.results[0]["out_0"]
```

```python
import concourse.bass as bass
from concourse import mybir
import numpy as np
from contextlib import ExitStack

F32 = mybir.dt.float32
BF16 = mybir.dt.bfloat16
I32 = mybir.dt.int32
ALU = mybir.AluOpType
ACT = mybir.ActivationFunctionType
AX_X = mybir.AxisListType.X

N = 50000
E = 50000
D = 64
P = 128
BLK = 256
Q = 4
WIN = Q * P
NB = -(-E // BLK)
NW = -(-N // WIN)
HALF_BLOCKS = NB // 2
HALF = HALF_BLOCKS * BLK
COLS = 2 * BLK
CHUNKS = HALF_BLOCKS // 2
SETS = 2 * (-(-(NB + NW) // 8))
EARLY = CHUNKS - 5
STEPS = 4 * SETS
R = D + 1
PAD_NODE = NW * WIN - 1
TAIL_E = E - (NB - 1) * BLK
TAIL_N = N - (NW - 1) * WIN
NODES = NW * Q
BATCH = NODES // CHUNKS
WB = BATCH // Q
INIT_TURNS = 8
BIG = 1.0e38
EPS = 1e-5


def constants():
    p = np.arange(P)
    ident = np.eye(P)
    node_of = np.zeros((P, Q, P))
    node_of[:] = (Q * p[None, :] + np.arange(Q)[:, None])[None] - WIN // 2
    shift = np.zeros((P, P))
    shift[p[:64], p[:64] + 64] = 1.0
    kept = np.concatenate([ident, shift], 1)
    i = np.arange(HALF_BLOCKS)
    order = np.stack([4 * (i // 2) + i % 2, 4 * (i // 2) + 2 + i % 2])
    setup = np.zeros((P, STEPS + 4 * HALF_BLOCKS + 2 + WIN))
    setup[:, :STEPS] = np.arange(STEPS)
    at = STEPS
    for h_from in range(2):
        for h_to in range(2):
            before = order[h_from][:, None] < order[h_to][None, :]
            setup[:HALF_BLOCKS, at:at + HALF_BLOCKS] = before
            at += HALF_BLOCKS
    for h in range(2):
        setup[:HALF_BLOCKS, at + h] = order[h]
    setup[:, at + 2:] = node_of.reshape(P, -1)
    return kept.astype(np.float32), setup.astype(np.float32)


def gnn_kernel(nc, x, src, dst, ef, ew, w0t, b0, w1t, b1, slope, kept_d, setup_d, out, rows_d, x1_d, hs_d):
    ctx = ExitStack()
    with ctx:
        def sb(name, shape, dt=F32):
            return ctx.enter_context(nc.sbuf_tensor(name, shape, dt))

        def sem(name):
            return ctx.enter_context(nc.semaphore(name))

        acc_t = sb("acc", [P, NODES * R])
        acc = acc_t[:, :].rearrange("p (w q r) -> p w q r", q=Q, r=R)
        accn = acc_t[:, :].rearrange("p (n r) -> p n r", r=R)
        kept = sb("kept", [P, 256])
        ident = kept[:, 0:128]
        shift = kept[:, 128:256]
        nident = sb("nident", [P, P])
        node_of16 = sb("node_of16", [P, WIN], BF16)
        minus_starts = sb("minus_starts", [P, COLS], BF16)
        spread = sb("spread", [2 * CHUNKS, CHUNKS, P], BF16)
        starts = sb("starts", [P, COLS], BF16)
        rel = sb("rel", [P, 2, STEPS])
        idx = sb("idx", [P, 2 * NB], I32)
        idx_h = sb("idx_h", [P, 2 * NB], I32)
        idx_now = [sb(f"idx_now{u}", [P, 8], I32) for u in range(4)]
        emit = sb("emit", [P, 2, 2, HALF_BLOCKS])
        ewe = sb("ewe", [P, 2, 2, HALF_BLOCKS])
        wtab = sb("wtab", [1, STEPS], I32)
        jtab = sb("jtab", [1, STEPS], I32)
        captab = sb("captab", [1, CHUNKS + 1], I32)
        w0 = sb("w0", [P, P])
        w1 = sb("w1", [P, P])
        b0r = sb("b0r", [P, R])
        b1r = sb("b1r", [P, D])
        slo = sb("slo", [P, 1])
        dinv = sb("dinv", [P, NODES])
        cap = sb("cap", [P, CHUNKS, 3])
        fixs = sb("fixs", [P, 16])
        fixf = sb("fixf", [1, D])
        fixrow = sb("fixrow", [P, 2, 3, R], BF16)
        onehot = sb("onehot", [P, 4, 2, WIN], BF16)
        steprow = sb("steprow", [P, 8, 2, 3, R], BF16)
        WORK = 14420
        work = sb("work", [P, WORK])

        class Carve:
            def __init__(self, t, end):
                self.t, self.at, self.end = t, 0, end

            def take(self, cols, parts=P):
                self.at += cols
                assert self.at <= self.end
                return self.t[0:parts, self.at - cols:self.at]

        HB = HALF_BLOCKS
        cs = Carve(acc_t, NODES * R)
        setc = cs.take(STEPS + 4 * HB + 2 + WIN)
        kf = setc[:, 0:STEPS]
        before = setc[0:HB, STEPS:STEPS + 4 * HB].rearrange("p (a b i) -> p a b i", a=2, b=2)
        order = setc[0:HB, STEPS + 4 * HB:STEPS + 4 * HB + 2]
        node_of = setc[:, STEPS + 4 * HB + 2:]
        nat = {}
        for nm in ("dst", "nxt", "src"):
            nat[nm + "i"] = cs.take(2 * BLK, HB).bitcast(I32)
            nat[nm] = cs.take(2 * BLK, HB)
        nat["ew"] = cs.take(2 * BLK, HB)
        dadj = cs.take(2 * BLK, HB)
        curi, prei = cs.take(COLS, 2 * CHUNKS).bitcast(I32), cs.take(COLS, 2 * CHUNKS).bitcast(I32)
        cur, pre = cs.take(COLS, 2 * CHUNKS), cs.take(COLS, 2 * CHUNKS)
        oh = cs.take(2 * STEPS, HB).rearrange("p (h k) -> p h k", h=2)
        oha = cs.take(2 * STEPS, HB).rearrange("p (h k) -> p h k", h=2)
        dste = cs.take(2 * NB).rearrange("p (t h i) -> p t h i", t=2, h=2)
        nxte = cs.take(2 * NB).rearrange("p (t h i) -> p t h i", t=2, h=2)
        crm = cs.take(2 * NB).rearrange("p (t h i) -> p t h i", t=2, h=2)
        fpi = cs.take(2, HB).bitcast(I32)
        fwi = cs.take(4, HB).bitcast(I32)
        fw = cs.take(4, HB)
        cnt = cs.take(2, HB)
        sst = cs.take(2, HB)
        sen = cs.take(2, HB)
        fms = cs.take(2, HB)
        fadj = cs.take(2, HB)
        crs = cs.take(1, HB)
        n0i = cs.take(1).bitcast(I32)
        n0 = cs.take(1)
        one = cs.take(1, HB)
        sc = cs.take(16, 1)
        sci = cs.take(4, 1).bitcast(I32)
        capf = cs.take(CHUNKS + 1, 1)
        rowf = cs.take(STEPS, 1)
        rowj = cs.take(STEPS, 1)
        idxf, quad_f, win_f = cs.take(2 * NB), cs.take(2 * NB), cs.take(2 * NB)
        quad, win = cs.take(2 * NB).bitcast(I32), cs.take(2 * NB).bitcast(I32)
        crj = cs.take(2 * BLK, HB)

        ca = Carve(work, WORK)
        g1 = [ca.take(8 * D) for _ in range(4)]
        m_s = [ca.take(COLS) for _ in range(2)]
        msa_w = [ca.take(3 * (COLS + 1)) for _ in range(2)]
        msa = [t.rearrange("p (a c) -> p a c", a=3) for t in msa_w]
        run_max, run_den, run_sum = [[t[:, a, :] for t in msa] for a in range(3)]
        ex = [ca.take(COLS) for _ in range(2)]
        dec = [ca.take(COLS) for _ in range(2)]
        mex = [ca.take(COLS) for _ in range(2)]
        rden = [ca.take(COLS) for _ in range(2)]
        q1 = [ca.take(COLS) for _ in range(2)]
        rows_w = [ca.take(8 * R) for _ in range(2)]
        rows = [t.rearrange("p (n r) -> p n r", r=R) for t in rows_w]
        parts_w = [ca.take(8 * 3 * R // 2).bitcast(BF16) for _ in range(2)]
        parts = [t.rearrange("p (n s r) -> p n s r", s=3, r=R) for t in parts_w]
        cb = Carve(work, WORK)
        xin = [cb.take(8 * D) for _ in range(4)]
        sq = [cb.take(8 * D) for _ in range(2)]
        x1s = [cb.take(8 * D) for _ in range(4)]
        hst = [cb.take(8 * D) for _ in range(2)]
        xds = [cb.take(8 * D) for _ in range(2)]
        xdt = [cb.take(8 * D) for _ in range(2)]
        var, mean, rstd, rdin = [cb.take(NODES) for _ in range(4)]
        g3 = [cb.take(8 * D) for _ in range(4)]
        rows3_w = [cb.take(8 * R) for _ in range(2)]
        parts3_w = [cb.take(8 * 3 * R // 2).bitcast(BF16) for _ in range(2)]
        rows3 = [t.rearrange("p (n r) -> p n r", r=R) for t in rows3_w]
        parts3 = [t.rearrange("p (n s r) -> p n s r", s=3, r=R) for t in parts3_w]

        moved = work[:, 6160:6160 + 8 * Q * R].rearrange("p (k q r) -> p k q r", q=Q, r=R)

        bank = [ctx.enter_context(nc.psum_tensor(f"bank{i}", [P, 512], F32)) for i in range(8)]
        m_p, n_p, q_p = bank[0:2], bank[2], bank[3]
        h_p = bank[2:4]

        names = """passed pads nat_d nat_s nat_w flags_d misc_d consts_d weights_d dch src_ready ppe0 ppe1 ppe2 cst16 sources
        tables acc_init tr m_ready colmax max_ready z_ready relu_ready exp_ready sum_ready mex_ready den_ready rc_ln
        rc_ready q_ready w_ready captured fix_row fix_pe fix_q fix_a fix_store deg_max dinv_sqrt z1 z z_sum z_cen z_sq
        z_sum2 z_var z_std z_rstd x1_t x1_tc hsp hs_out hs_acc x1m p3_clear o_sc o_b o_neg o_x o_z o_sum o_cen o_sq
        o_sum2 o_var o_std o_rstd o_out""".split()
        S = {n: sem("s_" + n) for n in names}
        ph = [{n: sem(f"s_{n}_{p}") for n in "rows_ready hi mid_in mid parts_ready built mm moved added".split()} for p in (1, 3)]
        for p, k in zip(ph, (1, 3)):
            p["stored"] = [sem(f"s_rows_stored{u}_{k}") for u in range(2)]
            p["steprow"] = [sem(f"s_steprow{u}_{k}") for u in range(8)]
        s_gath = [sem(f"s_gath{u}") for u in range(4)]
        s_idx = [sem(f"s_idx{u}") for u in range(4)]
        s_ef = [sem(f"s_ef{u}") for u in range(4)]
        s_xin = [sem(f"s_xin{u}") for u in range(4)]
        s_x1st = [sem(f"s_x1_stored{u}") for u in range(4)]
        s_hsst = [sem(f"s_hs_stored{u}") for u in range(2)]
        s_g3 = [sem(f"s_gath3_{u}") for u in range(4)]
        s_x1in = [sem(f"s_x1in{u}") for u in range(4)]
        s_outst = [sem(f"s_out_stored{u}") for u in range(4)]

        def held(eng):
            eng.sem_inc(S["passed"], 1)

        def first(c, ring=2):
            return isinstance(c, int) and c < ring

        def uses(u, ring=2):
            return -(-(CHUNKS - u) // ring)

        def staged(eng, *stages):
            stages = [(*st, CHUNKS)[:4] for st in stages]
            deep = max(lag for lag, _, _, _ in stages)
            assert all(lag + n >= CHUNKS // 4 * 4 for lag, _, _, n in stages)
            head = (deep + 7) // 4

            def turn(c, r, i):
                for lag, f, ring, n in stages:
                    if not isinstance(c, int) or 0 <= c - lag < n:
                        u = (r - lag) % ring
                        f(c - lag, u, (4 // ring) * i + (r - lag - u) // ring)
            for c in range(4 * head):
                turn(c, c % 4, c // 4)
            with eng.Fori(head, CHUNKS // 4) as i:
                for r in range(4):
                    turn(4 * i + r if r else 4 * i, r, i)
            for c in range(CHUNKS // 4 * 4, max(lag + n for lag, _, _, n in stages)):
                turn(c, c % 4, c // 4)

        def at(ap, i, n=1):
            return ap[:, bass.ds(i, n)]

        def uslot(n, v, alone):
            return bank[4 * v + n if alone else 4 + n][:, 0:Q * R].rearrange("p (q r) -> p q r", q=Q)

        def add(eng, instr, p, k, ready, sums):
            eng.wait_ge(p[ready], k + 1 - (4 * EARLY if ready == "moved" else 0))
            w = eng.value_load(at(wtab[0:1, :], k), min_val=0, max_val=NW - 1)
            cols = R if p is ph[0] else D
            a = acc[:, bass.ds(w, 1), :, 0:cols].rearrange("p w q r -> p (w q) r")
            if not (isinstance(k, int) and k == 0):
                eng.wait_ge(p["added"], k)
            instr.tensor_tensor(a, a, sums[:, :, 0:cols], ALU.add).then_inc(p["added"], 1)

        def load_step(eng, p, k, n, v):
            if isinstance(k, int) and k == STEPS - 1:
                j = NB
            else:
                held(eng)
                j = eng.value_load(at(jtab[0:1, :], k), min_val=0, max_val=NB - 1)
            eng.dma_start(steprow[:, 4 * v + n, :, :, :].rearrange("p t s r -> p (t s r)"),
                          rows_d[bass.ds(j * P, P), :]).then_inc(p["steprow"][4 * v + n], 16)

        def load_set(eng, p):
            def f(s, v, i):
                eng.wait_ge(p["stored"][v], 16 * (i + 1))
                held(eng)
                for n in range(4):
                    if not first(s):
                        eng.wait_ge(p["mm"], 4 * s + n - 7)
                    load_step(eng, p, 4 * s + n, n, v)
            return f

        def all_stored(eng, p):
            for u in range(2):
                eng.wait_ge(p["stored"][u], 16 * uses(u))


        def blocks_of(v, h, lo=0):
            base = h * HALF + lo
            full = HB if base + HB * BLK <= E else HB - 1
            main = v[base:base + full * BLK].rearrange("(i j) -> i j", j=BLK)
            rest = v[base + full * BLK:min(E, base + HB * BLK)] if full < HB else None
            return full, main, rest

        def win_view(a, b):
            return a[bass.ds(b * WB * WIN, WB * WIN), :].rearrange("(w p q) f -> p w (q f)", p=P, q=Q)

        def own_view(a, b):
            return a.rearrange("(p n) f -> p n f", p=P)[:, bass.ds(BATCH * b, BATCH), :]

        LAST = (CHUNKS - 1) * WB * WIN

        def full_windows(a):
            return a[LAST:LAST + (WB - 1) * WIN, :].rearrange("(w p q) f -> p w (q f)", p=P, q=Q)

        def short_window(a):
            return a[LAST + (WB - 1) * WIN:N, :].rearrange("(p q) f -> p (q f)", q=Q)

        block = ctx.enter_context(nc.Block())

        @block.sync
        def _(sp):
            sp.dma_start(kept[:, :], kept_d).then_inc(S["consts_d"], 16)
            sp.dma_start(setc, setup_d).then_inc(S["consts_d"], 16)
            sp.wait_ge(S["pads"], 1)
            for nm, v, lo, s in (("srci", src, 0, "nat_s"), ("dsti", dst, 0, "nat_d"), ("nxti", dst, 1, "nat_d"),
                                 ("ew", ew, 0, "nat_w")):
                for h in range(2):
                    full, main, rest = blocks_of(v, h, lo)
                    sp.dma_start(nat[nm][0:full, h * BLK:(h + 1) * BLK], main).then_inc(S[s], 16)
                    if rest is not None:
                        n = rest.shape[0]
                        sp.dma_start(nat[nm][full:full + 1, h * BLK:h * BLK + n],
                                     rest.rearrange("(a n) -> a n", a=1)).then_inc(S[s], 16)
            rows97 = 2 * CHUNKS - 1
            r = E - rows97 * COLS
            sp.dma_start(curi[0:rows97, :], dst[0:rows97 * COLS].rearrange("(a n) -> a n", n=COLS)).then_inc(S["flags_d"], 16)
            sp.dma_start(curi[rows97:rows97 + 1, 0:r],
                         dst[rows97 * COLS:E].rearrange("(a n) -> a n", a=1)).then_inc(S["flags_d"], 16)
            sp.dma_start(prei[0:1, 1:COLS], dst[0:COLS - 1].rearrange("(a n) -> a n", a=1)).then_inc(S["flags_d"], 16)
            sp.dma_start(prei[1:rows97, :],
                         dst[COLS - 1:rows97 * COLS - 1].rearrange("(a n) -> a n", n=COLS)).then_inc(S["flags_d"], 16)
            sp.dma_start(prei[rows97:rows97 + 1, 0:r],
                         dst[rows97 * COLS - 1:E - 1].rearrange("(a n) -> a n", a=1)).then_inc(S["flags_d"], 16)
            sp.dma_start(fpi[1:HB, 0:1], dst[BLK - 1:BLK - 1 + (HB - 1) * BLK].rearrange("(a n) -> a n", n=BLK)[:, 0:1], allow_slow_non_contiguous=True).then_inc(S["misc_d"], 16)
            sp.dma_start(fpi[0:HB, 1:2], dst.rearrange("(a n) -> a n", n=1)[HALF - 1:HALF + (HB - 1) * BLK:BLK, :], allow_slow_non_contiguous=True).then_inc(S["misc_d"], 16)
            sp.dma_start(n0i, dst[HALF - 1:HALF].rearrange("(a n) -> a n", a=1).broadcast_to([P, 1])).then_inc(S["misc_d"], 16)
            for t, d in ((w0, w0t), (w1, w1t)):
                for h in range(2):
                    sp.dma_start(t[h * D:(h + 1) * D, h * D:(h + 1) * D], d).then_inc(S["weights_d"], 16)
            sp.dma_start(b0r[:, 0:D], b0.rearrange("(a n) -> a n", a=1).broadcast_to([P, D])).then_inc(S["weights_d"], 16)
            sp.dma_start(b1r[:, :], b1.rearrange("(a n) -> a n", a=1).broadcast_to([P, D])).then_inc(S["weights_d"], 16)
            sp.dma_start(slo[:, :], slope.broadcast_to([P, 1])).then_inc(S["weights_d"], 16)

            def load_idx(c, u, table):
                sp.dma_start(idx_now[u][:, :], at(table[:, :], 8 * c, 8)).then_inc(s_idx[u], 16)

            def load_ef(c, u, i):
                if not first(c, 4):
                    sp.wait_ge(S["tr"], c - 3)
                for h in range(2):
                    d = g1[u].rearrange("p (n h f) -> p n h f", n=4, h=2)[:, :, h, :]
                    if isinstance(c, int) and c == CHUNKS - 1 and h == 1:
                        r0 = (NB - 2) * BLK
                        sp.dma_start(d[:, 0:2, :], ef[r0:r0 + BLK, :].rearrange("(n p) f -> p n f", p=P)).then_inc(s_ef[u], 16)
                        sp.dma_start(d[0:TAIL_E, 2:3, :].rearrange("p t f -> p (t f)"), ef[r0 + BLK:E, :]).then_inc(s_ef[u], 16)
                    else:
                        sp.dma_start(d, ef[bass.ds(c * COLS + h * HALF, COLS), :].rearrange("(n p) f -> p n f", p=P)).then_inc(s_ef[u], 16)
                if isinstance(c, int) and c == 0:
                    sp.wait_ge(S["sources"], 1)
                load_idx(c, u, idx)

            def store_rows(p, tiles):
                def f(c, u, i):
                    sp.wait_ge(p["parts_ready"], c + 1)
                    dview = rows_d[bass.ds(c * 4 * P, 4 * P), :].rearrange("(j p) f -> p j f", p=P)
                    sp.dma_start(dview, tiles[u].rearrange("p (j f) -> p j f", j=4)).then_inc(p["stored"][u], 16)
                return f

            def late_sets(p):
                all_stored(sp, p)
                with sp.Fori(EARLY // 2, SETS // 2) as i:
                    for v in range(2):
                        for n in (0, 2):
                            sp.wait_ge(p["mm"], 8 * i + 4 * v + n - 7)
                            load_step(sp, p, 8 * i + 4 * v + n, n, v)

            def wait_tables(c, u, i):
                if isinstance(c, int) and c == 0:
                    sp.wait_ge(S["tables"], 1)
            staged(sp, (7, store_rows(ph[0], parts_w), 2), (0, load_ef, 4), (8, wait_tables, 2), (8, load_set(sp, ph[0]), 2, EARLY))
            sp.wait_ge(S["fix_row"], 1)
            sp.dma_start(rows_d[NB * P:(NB + 1) * P, :], fixrow[:, :, :, :].rearrange("p t s r -> p (t s r)")).then_inc(S["fix_store"], 16)
            late_sets(ph[0])

            def load_x(b, u, i):
                if not first(b, 4):
                    sp.wait_ge(S["z"], b - 3)
                tv = xin[u].rearrange("p (w f) -> p w f", w=WB)
                if isinstance(b, int) and b == CHUNKS - 1:
                    sp.dma_start(tv[:, 0:WB - 1, :], full_windows(x)).then_inc(s_xin[u], 16)
                    sp.dma_start(tv[0:TAIL_N // Q, WB - 1, :], short_window(x)).then_inc(s_xin[u], 16)
                else:
                    sp.dma_start(tv, win_view(x, b)).then_inc(s_xin[u], 16)

            def store_x1(b, u, i):
                sp.wait_ge(S["x1m"], b + 1)
                sp.dma_start(own_view(x1_d, b), x1s[u].rearrange("p (n f) -> p n f", f=D)).then_inc(s_x1st[u], 16)

            def store_h(b, u, i):
                sp.wait_ge(S["hs_out"], b + 1)
                sp.dma_start(own_view(hs_d, b), hst[u].rearrange("p (n f) -> p n f", f=D)).then_inc(s_hsst[u], 16)

            sp.wait_ge(ph[0]["added"], STEPS)
            staged(sp, (8, store_x1, 4), (11, store_h, 2), (0, load_x, 4))

            def next_idx(c, u, i):
                if not first(c, 4):
                    sp.wait_ge(ph[1]["hi"], c - 3)
                load_idx(c, u, idx_h)
            staged(sp, (5, store_rows(ph[1], parts3_w), 2), (0, next_idx, 4), (6, load_set(sp, ph[1]), 2, EARLY))
            late_sets(ph[1])

            for u in range(4):
                sp.wait_ge(s_x1st[u], 16 * uses(u, 4))
            sp.wait_ge(ph[1]["added"], 4 * EARLY)

            def load_x1(b, u, i):
                if not first(b, 4):
                    sp.wait_ge(S["o_x"], b - 3)
                sp.dma_start(xin[u].rearrange("p (n f) -> p n f", f=D), own_view(x1_d, b)).then_inc(s_x1in[u], 16)

            def store_out(b, u, i):
                sp.wait_ge(S["o_out"], b + 1)
                tv = x1s[u].rearrange("p (w f) -> p w f", w=WB)
                if isinstance(b, int) and b == CHUNKS - 1:
                    sp.dma_start(full_windows(out), tv[:, 0:WB - 1, :]).then_inc(s_outst[u], 16)
                    sp.dma_start(short_window(out), tv[0:TAIL_N // Q, WB - 1, :]).then_inc(s_outst[u], 16)
                else:
                    sp.dma_start(win_view(out, b), tv).then_inc(s_outst[u], 16)
            staged(sp, (10, store_out, 4), (0, load_x1, 4))
            for u in range(4):
                sp.wait_ge(s_outst[u], 16 * (uses(u, 4) + (1 if u == (CHUNKS - 1) % 4 else 0)))

        @block.gpsimd
        def _(pool):
            def gather1(c, u, i):
                pool.wait_ge(s_idx[u], 16 * (i + 1))
                pool.wait_ge(s_ef[u], 32 * (i + 1) + (16 if isinstance(c, int) and c == CHUNKS - 1 else 0))
                held(pool)
                for h in range(2):
                    for b in range(2):
                        for t in range(2):
                            n, o = (2 * h + b) * 2 + t, ((2 * b + t) * 2 + h) * D
                            nc.gpsimd.indirect_dma_start(
                                g1[u][:, o:o + D], None, x[:, :],
                                bass.IndirectOffsetOnAxis(ap=idx_now[u][:, n:n + 1], axis=0),
                                compute_op=ALU.add).then_inc(s_gath[u], 16)
            staged(pool, (0, gather1, 4))

            def late_adds(p):
                with pool.Fori(EARLY // 2, SETS // 2) as i:
                    for v in range(2):
                        for n in range(4):
                            add(pool, nc.gpsimd, p, 8 * i + 4 * v + n, "moved", moved[:, 4 * v + n])
            late_adds(ph[0])

            def nodes(b):
                return accn[:, bass.ds(8 * b, 8), 0:D]

            def by_node(t, b):
                return t[:, bass.ds(8 * b, 8)].unsqueeze(2).broadcast_to([P, 8, D])

            def add_x(b, u, i):
                pool.wait_ge(S["z1"], b + 1)
                nc.gpsimd.tensor_tensor(nodes(b), nodes(b), xin[u].rearrange("p (n f) -> p n f", f=D), ALU.add).then_inc(S["z"], 1)

            def x1_mul(b, u, i):
                pool.wait_ge(S["z_rstd"], b + 1)
                if not first(b, 4):
                    pool.wait_ge(s_x1st[u], 16 * i)
                    pool.wait_ge(S["x1_t"], b - 3)
                nc.gpsimd.tensor_tensor(x1s[u].rearrange("p (n f) -> p n f", f=D), nodes(b), by_node(rstd, b), ALU.mult).then_inc(S["x1m"], 1)
            staged(pool, (0, add_x, 4), (6, x1_mul, 4))

            for u in range(2):
                pool.wait_ge(s_hsst[u], 16 * uses(u))

            def gather3(c, u, i):
                pool.wait_ge(s_idx[u], 16 * (uses(u, 4) + i + 1))
                held(pool)
                for n in range(8):
                    nc.gpsimd.indirect_dma_start(g3[u][:, n * D:(n + 1) * D], None, hs_d[:, :],
                        bass.IndirectOffsetOnAxis(ap=idx_now[u][:, n:n + 1], axis=0)).then_inc(s_g3[u], 16)
            staged(pool, (0, gather3, 4))
            late_adds(ph[1])

            def add_bias(b, u, i):
                pool.wait_ge(S["o_sc"], b + 1)
                nc.gpsimd.tensor_tensor(nodes(b), nodes(b), b1r[:, :].unsqueeze(1).broadcast_to([P, 8, D]), ALU.add).then_inc(S["o_b"], 1)

            def add_x1(b, u, i):
                pool.wait_ge(S["o_neg"], b + 1)
                pool.wait_ge(s_x1in[u], 16 * (i + 1))
                nc.gpsimd.tensor_tensor(xds[u % 2], xds[u % 2], xin[u], ALU.add).then_inc(S["o_x"], 1)

            def out_mul(b, u, i):
                pool.wait_ge(S["o_rstd"], b + 1)
                if not first(b, 4):
                    pool.wait_ge(s_outst[u], 16 * i)
                nc.gpsimd.tensor_tensor(x1s[u].rearrange("p (n f) -> p n f", f=D), nodes(b), by_node(rstd, b), ALU.mult).then_inc(S["o_out"], 1)
            staged(pool, (1, add_bias, 2), (3, add_x1, 4), (8, out_mul, 4))

        @block.scalar
        def _(act):
            act.wait_ge(S["tables"], 1)
            act.wait_ge(S["weights_d"], 16 * 7)
            nc.scalar.preload_act_table_set("natural_log_exp_and_others")

            def copy_m(c, u, i):
                act.wait_ge(S["tr"], c + 1)
                if not first(c):
                    act.wait_ge(S["mex_ready"], c - 1)
                nc.scalar.activation(m_s[u], m_p[u][:, :], ACT.Copy).then_inc(S["m_ready"], 1)

            def recip(c, u, i):
                act.wait_ge(S["den_ready"], c + 1)
                if not first(c):
                    act.wait_ge(S["q_ready"], c - 1)
                nc.scalar.activation(rden[u], run_den[u][:, 1:], ACT.Ln).then_inc(S["rc_ln"], 1)
                act.wait_ge(S["rc_ln"], c + 1)
                nc.scalar.activation(rden[u], rden[u], ACT.Exp, scale=-1.0).then_inc(S["rc_ready"], 1)

            def exps(c, u, i):
                act.wait_ge(S["z_ready"], c + 1)
                if not first(c):
                    act.wait_ge(S["sum_ready"], c - 1)
                nc.scalar.activation(dec[u], m_p[u][:, :], ACT.Relu)
                nc.scalar.activation(ex[u], m_p[u][:, :], ACT.Relu, scale=-1.0).then_inc(S["relu_ready"], 1)
                act.wait_ge(S["relu_ready"], c + 1)
                nc.scalar.activation(dec[u], dec[u], ACT.Exp, scale=-1.0)
                nc.scalar.activation(ex[u], ex[u], ACT.Exp, scale=-1.0).then_inc(S["exp_ready"], 1)

            def high_part(p, r, t, u, c):
                act.wait_ge(p["rows_ready"], c + 1)
                nc.scalar.activation(t[u][:, :, 0, :], r[u][:, :, :], ACT.Copy).then_inc(p["hi"], 1)

            def middle_part(p, r, t):
                def f(c, u, i):
                    act.wait_ge(p["mid_in"], c + 1)
                    nc.scalar.activation(t[u][:, :, 1, :], r[u][:, :, :], ACT.Copy).then_inc(p["mid"], 1)
                return f

            def mask_rows(c, u, i):
                act.wait_ge(S["w_ready"], c + 1)
                if not first(c):
                    act.wait_ge(ph[0]["stored"][u], 16 * i)
                held(act)
                for h in range(2):
                    for b in range(2):
                        for t in range(2):
                            o = ((2 * b + t) * 2 + h) * D
                            nc.scalar.activation(rows[u][:, (2 * h + b) * 2 + t, 0:D], q_p[:, o:o + D], ACT.Copy,
                                                 scale=at(emit[:, t, h, :], 2 * c + b))
                    last = nc.scalar.activation(rows[u].rearrange("p (h b t) r -> p h b t r", h=2, b=2)[:, h, :, :, D],
                                                ewe[:, :, h, bass.ds(2 * c, 2)].rearrange("p t b -> p b t"), ACT.Copy)
                last.then_inc(ph[0]["rows_ready"], 1)
                high_part(ph[0], rows, parts, u, c)

            def capture(c, u, i):
                act.wait_ge(S["sum_ready"], c + 1)
                held(act)
                col = act.value_load(at(captab[0:1, :], c), min_val=0, max_val=COLS - 1)
                nc.scalar.activation(cap[:, bass.ds(c, 1), :].rearrange("p c a -> p a c"), msa[u][:, :, bass.ds(1 + col, 1)], ACT.Copy).then_inc(S["captured"], 1)

            def init_sums(c, u, i):
                if isinstance(c, int) and c < INIT_TURNS:
                    n = NODES // INIT_TURNS
                    nc.scalar.activation(accn[:, c * n:(c + 1) * n, :], b0r[:, :].unsqueeze(1).broadcast_to([P, n, R]), ACT.Copy).then_inc(S["acc_init"], 1)

            staged(act, (2, recip, 2), (1, exps, 2), (4, middle_part(ph[0], rows, parts), 2), (0, copy_m, 2), (3, mask_rows, 2), (1, capture, 2), (0, init_sums, 2))
            act.wait_ge(S["fix_q"], 1)
            nc.scalar.activation(fixs[:, 9:11], fixs[:, 7:9], ACT.Exp).then_inc(S["fix_a"], 1)

            def late_moves(p):
                act.wait_ge(p["added"], 4 * EARLY)
                all_stored(act, p)
                cols = R if p is ph[0] else D
                for v in range(2):
                    for n in (1, 3):
                        load_step(act, p, 4 * (EARLY + v) + n, n, v)

                def two_sets(i, last):
                    for v in range(2):
                        for n in range(4):
                            k = 8 * i + 4 * v + n
                            act.wait_ge(p["mm"], k + 1)
                            act.wait_ge(p["added"], k - 7)
                            nc.scalar.activation(moved[:, 4 * v + n, :, 0:cols], uslot(n, v, True)[:, :, 0:cols], ACT.Copy).then_inc(p["moved"], 1)
                            if n % 2 and not last:
                                load_step(act, p, k + 8, n, v)
                with act.Fori(EARLY // 2, SETS // 2 - 2) as i:
                    two_sets(i, False)
                act.wait_ge(S["fix_store"], 16)
                two_sets(SETS // 2 - 2, False)
                two_sets(SETS // 2 - 1, True)
            late_moves(ph[0])

            nc.scalar.preload_act_table_set("sqrt_and_others")
            act.wait_ge(S["deg_max"], 1)
            nc.scalar.activation(dinv[:, :], dinv[:, :], ACT.Sqrt).then_inc(S["dinv_sqrt"], 1)

            def square(cen, sum2, done):
                def f(b, u, i):
                    act.wait_ge(S[cen], b + 1)
                    if not first(b):
                        act.wait_ge(S[sum2], b - 1)
                    held(act)
                    nc.scalar.activation(sq[u].rearrange("p (n f) -> p n f", f=D), accn[:, bass.ds(8 * b, 8), 0:D], ACT.Square).then_inc(S[done], 1)
                return f

            def deviation(var_ready, done):
                def f(b, u, i):
                    act.wait_ge(S[var_ready], b + 1)
                    held(act)
                    nc.scalar.activation(at(rstd, 8 * b, 8), at(var, 8 * b, 8), ACT.Sqrt).then_inc(S[done], 1)
                return f

            def evac2(b, u, i):
                act.wait_ge(S["x1_t"], b + 1)
                if not first(b):
                    act.wait_ge(S["hsp"], b - 1)
                nc.scalar.activation(xdt[u], m_p[u][:, :], ACT.Copy).then_inc(S["x1_tc"], 1)

            def scale_h(b, u, i):
                act.wait_ge(S["hsp"], b + 1)
                if not first(b):
                    act.wait_ge(s_hsst[u], 16 * i)
                    act.wait_ge(S["hs_acc"], b - 1)
                held(act)
                for n in range(BATCH):
                    last = nc.scalar.activation(hst[u][:, n * D:(n + 1) * D], h_p[u][:, n * D:(n + 1) * D], ACT.Copy,
                                                scale=at(dinv[:, :], BATCH * b + n))
                last.then_inc(S["hs_out"], 1)
            staged(act, (2, square("z_cen", "z_sum2", "z_sq"), 2), (8, evac2, 2), (4, deviation("z_var", "z_std"), 2), (9, scale_h, 2))

            def weight_rows(c, u, i):
                act.wait_ge(s_g3[u], 128 * (i + 1))
                v, before = u % 2, 2 * i + u // 2
                if not first(c):
                    act.wait_ge(ph[1]["stored"][v], 16 * before)
                held(act)
                for h in range(2):
                    for b in range(2):
                        for t in range(2):
                            n = (2 * h + b) * 2 + t
                            last = nc.scalar.activation(rows3[v][:, n, 0:D], g3[u][:, n * D:(n + 1) * D], ACT.Copy,
                                                        scale=at(ewe[:, t, h, :], 2 * c + b))
                last.then_inc(ph[1]["rows_ready"], 1)
                high_part(ph[1], rows3, parts3, v, c)
            act.wait_ge(S["p3_clear"], 1)
            staged(act, (2, middle_part(ph[1], rows3, parts3), 2), (1, weight_rows, 4))
            late_moves(ph[1])

            act.wait_ge(ph[1]["added"], STEPS)
            held(act)

            def scale_sum(b, u, i):
                for n in range(BATCH):
                    o = at(accn, BATCH * b + n)[:, :, 0:D]
                    last = nc.scalar.activation(o, o, ACT.Copy, scale=at(dinv[:, :], BATCH * b + n))
                last.then_inc(S["o_sc"], 1)
            staged(act, (0, scale_sum, 2), (5, square("o_cen", "o_sum2", "o_sq"), 2), (6, deviation("o_var", "o_std"), 2))

        @block.vector
        def _(dve):
            chain = [0]

            def link(ins):
                chain[0] += 1
                ins.then_inc(S["dch"], 1)
                dve.wait_ge(S["dch"], chain[0])

            V = nc.vector
            V.memset(nat["srci"], 0)
            V.memset(nat["dsti"], PAD_NODE)
            V.memset(nat["nxti"], PAD_NODE + 1)
            V.memset(nat["ew"], 0.0)
            V.memset(curi, PAD_NODE)
            V.memset(prei, -1)
            V.memset(fpi, 0)
            V.memset(w0[:, :], 0.0)
            V.memset(w1[:, :], 0.0)
            V.memset(b0r[:, :], 1.0)
            V.memset(one, 1.0)
            V.memset(fixrow[:, :, :, :], 0.0)
            V.memset(run_max[1][:, COLS:], -BIG)
            V.memset(run_den[1][:, COLS:], 0.0)
            V.memset(run_sum[1][:, COLS:], 0.0).then_inc(S["pads"], 1)
            dve.wait_ge(S["consts_d"], 32)
            V.tensor_copy(node_of16[:, :], node_of)
            dve.wait_ge(S["nat_s"], 16 * 3)
            V.tensor_copy(nat["src"], nat["srci"]).then_inc(S["src_ready"], 1)
            dve.wait_ge(S["ppe0"], 1)
            for t in range(2):
                for h in range(2):
                    V.tensor_copy(idx[:, :].rearrange("p (c h b t) -> p h t c b", h=2, b=2, t=2)[:, h, t, :, :],
                                  bank[2][:, (2 * t + h) * HB:(2 * t + h + 1) * HB].rearrange("p (c b) -> p c b", b=2))
            V.memset(sc[:, 14:15], 0.0).then_inc(S["sources"], 1)
            dve.wait_ge(S["nat_d"], 16 * 6)
            dve.wait_ge(S["nat_w"], 16 * 3)
            dve.wait_ge(S["flags_d"], 16 * 5)
            dve.wait_ge(S["misc_d"], 16 * 3)
            for nm in ("dst", "nxt"):
                V.tensor_copy(nat[nm], nat[nm + "i"])
            V.tensor_copy(cur, curi)
            V.tensor_copy(pre, prei)
            V.tensor_copy(n0, n0i)
            for h in range(2):
                V.tensor_copy(spread[:, :, h * D:(h + 1) * D],
                              ident[0:2 * CHUNKS, h * CHUNKS:(h + 1) * CHUNKS].unsqueeze(2).broadcast_to([2 * CHUNKS, CHUNKS, D]))
            V.tensor_scalar(nident[:, :], ident, -1.0, None, ALU.mult)
            V.tensor_copy(fwi[:, 0:2], fpi)
            link(V.tensor_copy(fwi[:, 2:4], nat["dsti"].rearrange("p (h j) -> p h j", h=2)[:, :, BLK - 1]))
            link(V.tensor_single_scalar(fwi, fwi, 9, ALU.arith_shift_right))
            link(V.tensor_copy(fw, fwi))
            link(V.tensor_tensor(cnt, fw[:, 2:4], fw[:, 0:2], ALU.subtract))
            link(V.tensor_scalar(cnt, cnt, 1.0, None, ALU.add))
            link(V.tensor_scalar(crj[:, 0:BLK], nat["dst"][:, BLK:2 * BLK], n0[0:HB, :], 0.0, ALU.is_equal, ALU.add, accum_out=crs))
            link(V.tensor_tensor(cur, cur, pre, ALU.is_equal))
            V.tensor_scalar(minus_starts[0:2 * CHUNKS, :], cur, -1.0, -BIG, ALU.add, ALU.mult)
            V.tensor_scalar(starts[0:2 * CHUNKS, :], cur, -1.0, BIG, ALU.add, ALU.mult).then_inc(S["cst16"], 1)
            dve.wait_ge(S["ppe1"], 1)
            V.tensor_copy(dste.rearrange("p t h i -> p (t h i)"), bank[0][:, 0:2 * NB])
            V.tensor_copy(nxte.rearrange("p t h i -> p (t h i)"), bank[1][:, 0:2 * NB])
            V.tensor_copy(ewe[:, :, :, :].rearrange("p t h i -> p (t h i)"), bank[3][:, 0:2 * NB])
            V.tensor_copy(sst, bank[4][0:HB, 0:2])
            link(V.tensor_copy(sc[:, 0:1], bank[5][0:1, 0:1]))
            V.tensor_tensor(emit[:, :, :, :].rearrange("p t h i -> p (t h i)"), dste.rearrange("p t h i -> p (t h i)"),
                            nxte.rearrange("p t h i -> p (t h i)"), ALU.not_equal)
            link(V.tensor_scalar(crm[:, :, 1, :], dste[:, :, 1, :], n0, None, ALU.not_equal))
            link(V.tensor_tensor(emit[:, :, 1, :], emit[:, :, 1, :], crm[:, :, 1, :], ALU.mult))
            V.tensor_tensor(fms, fw[:, 0:2], sst, ALU.subtract)
            link(V.tensor_tensor(sen, sst, cnt, ALU.add))
            link(V.tensor_scalar(fadj, fms, -float(WIN), -float(WIN // 2), ALU.mult, ALU.add))
            for h in range(2):
                V.tensor_scalar(oha[:, h, :], kf[0:HB, :], sst[:, h:h + 1], None, ALU.is_ge)
                V.tensor_scalar(dadj[:, h * BLK:(h + 1) * BLK], nat["dst"][:, h * BLK:(h + 1) * BLK], fadj[:, h:h + 1], None, ALU.add)
            link(V.tensor_copy(sc[:, 1:2], n0[0:1, :]))
            for h in range(2):
                last = V.scalar_tensor_tensor(oh[:, h, :], kf[0:HB, :], sen[:, h:h + 1], oha[:, h, :], ALU.is_lt, ALU.mult)
            link(last)
            V.tensor_copy(sci[:, 0:1], n0i[0:1, :]).then_inc(S["cst16"], 1)
            dve.wait_ge(S["cst16"], 2)
            link(V.tensor_single_scalar(sci[:, 0:1], sci[:, 0:1], 9, ALU.arith_shift_right))
            V.tensor_copy(sc[:, 4:5], sci[:, 0:1])
            V.tensor_scalar(sc[:, 2:3], sc[:, 0:1], 1.0, None, ALU.is_ge)
            link(V.tensor_scalar(sc[:, 3:4], sc[:, 0:1], -1.0, 0.0, ALU.add, ALU.max))
            link(V.tensor_scalar(sc[:, 6:7], sc[:, 4:5], -float(WIN), 1.0, ALU.mult, ALU.add))
            link(V.tensor_tensor(sc[:, 5:6], sc[:, 6:7], sc[:, 1:2], ALU.add))
            link(V.tensor_tensor(sc[:, 5:6], sc[:, 5:6], sc[:, 2:3], ALU.mult))
            link(V.tensor_scalar(capf, kf[0:1, 0:CHUNKS + 1], -float(COLS), sc[:, 3:4], ALU.mult, ALU.add))
            link(V.tensor_scalar(capf, capf, 0.0, float(COLS - 1), ALU.max, ALU.min))
            V.tensor_copy(captab[:, :], capf)
            link(V.tensor_copy(sci[:, 1:2], sc[:, 3:4]))
            link(V.tensor_single_scalar(sci[:, 1:2], sci[:, 1:2], 9, ALU.arith_shift_right))
            V.tensor_copy(captab[:, CHUNKS:CHUNKS + 1], sci[:, 1:2])
            dve.wait_ge(S["ppe2"], 1)
            for t in range(2):
                V.scalar_tensor_tensor(rel[:, t, :], kf, -float(WIN), bank[t][:, 0:STEPS], ALU.mult, ALU.add)
            V.tensor_tensor(rowf, bank[4][0:1, 0:STEPS], kf[0:1, :], ALU.add)
            V.tensor_copy(rowj, bank[5][0:1, 0:STEPS])
            link(V.tensor_scalar(sc[:, 7:8], sc[:, 5:6], -1.0 - WIN // 2, None, ALU.add))
            V.tensor_copy(rel[0:1, 0, STEPS - 1:], sc[:, 7:8])
            V.tensor_copy(rowf[:, STEPS - 1:], sc[:, 4:5])
            link(V.memset(rowj[:, STEPS - 1:], float(NB - 1)))
            link(V.tensor_scalar(rowf, rowf, float(NW - 1), None, ALU.min))
            V.tensor_copy(wtab[:, :], rowf)
            V.tensor_copy(jtab[:, :], rowj)
            V.tensor_single_scalar(quad, idx[:, :], 2, ALU.arith_shift_right)
            V.tensor_single_scalar(win, idx[:, :], 9, ALU.arith_shift_right)
            link(V.tensor_copy(idxf, idx[:, :]))
            V.tensor_copy(quad_f, quad)
            link(V.tensor_copy(win_f, win))
            link(V.scalar_tensor_tensor(idxf, quad_f, float(NODES - Q), idxf, ALU.mult, ALU.add))
            link(V.scalar_tensor_tensor(idxf, win_f, float(Q - P * NODES), idxf, ALU.mult, ALU.add))
            link(V.tensor_copy(idx_h[:, :], idxf))
            V.memset(sc[:, 15:16], 0.0).then_inc(S["tables"], 1)

            def build(p, n):
                def f(s, v, i):
                    if not (isinstance(s, int) and s == 0):
                        dve.wait_ge(p["mm"], 4 * s + n - 3)
                    for t in range(2):
                        last = V.tensor_scalar(onehot[:, n, t, :], node_of16[:, :], at(rel[:, t, :], 4 * s + n), None, ALU.is_equal)
                    last.then_inc(p["built"], 1)
                return f

            def add_step(p, n):
                def f(s, v, i):
                    if p is ph[0] and n == 0 and isinstance(s, int) and s == 0:
                        dve.wait_ge(S["acc_init"], INIT_TURNS)
                    add(dve, V, p, 4 * s + n, "mm", uslot(n, v, False))
                return f

            def steps_of(p, lag):
                return [st for n in range(4) for st in ((lag + 1, add_step(p, n), 2, EARLY), (lag, build(p, n), 2, EARLY))]

            def late_sets(p):
                with dve.Fori(EARLY, SETS) as s:
                    for n in range(4):
                        dve.wait_ge(p["mm"], 4 * s + n - 3)
                        for t in range(2):
                            last = V.tensor_scalar(onehot[:, n, t, :], node_of16[:, :], at(rel[:, t, :], 4 * s + n), None, ALU.is_equal)
                        last.then_inc(p["built"], 1)

            def after_high(p, r, t):
                def f(c, u, i):
                    dve.wait_ge(p["hi"], c + 1)
                    V.tensor_tensor(r[u][:, :, :], r[u][:, :, :], t[u][:, :, 0, :], ALU.subtract).then_inc(p["mid_in"], 1)
                return f

            def low_part(p, r, t):
                def f(c, u, i):
                    dve.wait_ge(p["mid"], c + 1)
                    V.tensor_tensor(t[u][:, :, 2, :], r[u][:, :, :], t[u][:, :, 1, :], ALU.subtract).then_inc(p["parts_ready"], 1)
                return f

            def scan_max(c, u, i):
                dve.wait_ge(S["m_ready"], c + 1)
                if not (isinstance(c, int) and c == 0):
                    dve.wait_ge(S["max_ready"], c)
                if not first(c):
                    dve.wait_ge(S["z_ready"], c - 1)
                    dve.wait_ge(S["captured"], c - 1)
                V.tensor_copy(run_max[u][:, 0:1], run_max[1 - u][:, COLS:]).then_inc(S["colmax"], 1)
                dve.wait_ge(S["colmax"], c + 1)
                V.tensor_tensor_scan(run_max[u][:, 1:], n_p[:, :], m_s[u], run_max[u][:, 0:1], ALU.add, ALU.max).then_inc(S["max_ready"], 1)

            def scan_sums(c, u, i):
                dve.wait_ge(S["exp_ready"], c + 1)
                if not first(c):
                    dve.wait_ge(S["rc_ready"], c - 1)
                if not (isinstance(c, int) and c == 0):
                    dve.wait_ge(S["sum_ready"], c)
                V.tensor_tensor_scan(run_den[u][:, 1:], dec[u], ex[u], run_den[1 - u][:, COLS:], ALU.mult, ALU.add).then_inc(S["den_ready"], 1)
                V.tensor_tensor(mex[u], m_s[u], ex[u], ALU.mult).then_inc(S["mex_ready"], 1)
                dve.wait_ge(S["mex_ready"], c + 1)
                V.tensor_tensor_scan(run_sum[u][:, 1:], dec[u], mex[u], run_sum[1 - u][:, COLS:], ALU.mult, ALU.add).then_inc(S["sum_ready"], 1)

            def quotient(c, u, i):
                dve.wait_ge(S["rc_ready"], c + 1)
                dve.wait_ge(S["sum_ready"], c + 1)
                if not first(c):
                    dve.wait_ge(S["w_ready"], c - 1)
                V.scalar_tensor_tensor(q1[u], rden[u], 1.0e38, run_sum[u][:, 1:], ALU.min, ALU.mult).then_inc(S["q_ready"], 1)

            staged(dve, *steps_of(ph[0], 7), (4, low_part(ph[0], rows, parts), 2), (2, quotient, 2),
                   (1, scan_sums, 2), (0, scan_max, 2), (3, after_high(ph[0], rows, parts), 2))

            def fix_crossing():
                dve.wait_ge(S["captured"], CHUNKS)
                cc = dve.value_load(captab[0:1, CHUNKS:CHUNKS + 1], min_val=0, max_val=CHUNKS - 1)
                V.tensor_copy(fixs[:, 3:6], cap[:, bass.ds(cc, 1), :].rearrange("p c a -> p (c a)"))
                dve.wait_ge(S["fix_pe"], 1)
                link(V.tensor_copy(fixs[:, 0:3], bank[7][:, 400:403]))
                link(V.tensor_tensor(fixs[:, 6:7], fixs[:, 0:1], fixs[:, 3:4], ALU.max))
                V.tensor_tensor(fixs[:, 7:8], fixs[:, 0:1], fixs[:, 6:7], ALU.subtract)
                V.tensor_tensor(fixs[:, 8:9], fixs[:, 3:4], fixs[:, 6:7], ALU.subtract).then_inc(S["fix_q"], 1)
                dve.wait_ge(S["fix_a"], 1)
                V.tensor_scalar(fixs[:, 1:3], fixs[:, 1:3], fixs[:, 9:10], None, ALU.mult)
                link(V.tensor_scalar(fixs[:, 4:6], fixs[:, 4:6], fixs[:, 10:11], None, ALU.mult))
                link(V.tensor_tensor(fixs[:, 1:3], fixs[:, 1:3], fixs[:, 4:6], ALU.add))
                link(V.tensor_scalar(fixs[:, 1:2], fixs[:, 1:2], 1.0e-38, None, ALU.max))
                link(V.reciprocal(fixs[:, 1:2], fixs[:, 1:2]))
                V.tensor_tensor(fixs[:, 11:12], fixs[:, 1:2], fixs[:, 2:3], ALU.mult).then_inc(S["fix_q"], 1)
                dve.wait_ge(S["fix_pe"], 2)
                link(V.tensor_copy(fixf[:, :], bank[7][0:1, D:2 * D]))
                for part in range(2):
                    link(V.tensor_copy(fixrow[0:1, 0, part, 0:D], fixf[:, :]))
                    link(V.tensor_tensor(fixf[:, :], fixf[:, :], fixrow[0:1, 0, part, 0:D], ALU.subtract))
                V.tensor_copy(fixrow[0:1, 0, 2, 0:D], fixf[:, :]).then_inc(S["fix_row"], 1)
            fix_crossing()
            late_sets(ph[0])

            dve.wait_ge(ph[0]["added"], STEPS)
            V.tensor_scalar(dinv[:, :], accn[:, :, D], 1.0e-12, None, ALU.max).then_inc(S["deg_max"], 1)
            V.tensor_scalar(rdin, accn[:, :, D], 0.0, None, ALU.is_gt)
            dve.wait_ge(S["dinv_sqrt"], 1)
            link(V.reciprocal(dinv[:, :], dinv[:, :]))
            link(V.tensor_tensor(dinv[:, :], dinv[:, :], rdin, ALU.mult))

            def nodes(b):
                return accn[:, bass.ds(8 * b, 8), 0:D]

            def by_node(t, b):
                return t[:, bass.ds(8 * b, 8)].unsqueeze(2).broadcast_to([P, 8, D])

            def relu_x(b, u, i):
                dve.wait_ge(s_xin[u], 16 * (i + 1) + (16 if isinstance(b, int) and b == CHUNKS - 1 else 0))
                V.scalar_tensor_tensor(nodes(b), nodes(b), 0.0, xin[u].rearrange("p (n f) -> p n f", f=D), ALU.max, ALU.add).then_inc(S["z1"], 1)

            def centre(ready, summed, done):
                def f(b, u, i):
                    dve.wait_ge(S[ready], b + 1)
                    V.reduce_sum(at(mean, 8 * b, 8), nodes(b), AX_X).then_inc(S[summed], 1)
                    dve.wait_ge(S[summed], b + 1)
                    V.scalar_tensor_tensor(nodes(b), by_node(mean, b), -1.0 / D, nodes(b), ALU.mult, ALU.add).then_inc(S[done], 1)
                return f

            def variance(ready, summed, done):
                def f(b, u, i):
                    dve.wait_ge(S[ready], b + 1)
                    V.reduce_sum(at(var, 8 * b, 8), sq[u].rearrange("p (n f) -> p n f", f=D), AX_X).then_inc(S[summed], 1)
                    dve.wait_ge(S[summed], b + 1)
                    V.tensor_scalar(at(var, 8 * b, 8), at(var, 8 * b, 8), 1.0 / D, EPS, ALU.mult, ALU.add).then_inc(S[done], 1)
                return f

            def inverse(ready, done):
                def f(b, u, i):
                    dve.wait_ge(S[ready], b + 1)
                    V.reciprocal(at(rstd, 8 * b, 8), at(rstd, 8 * b, 8)).then_inc(S[done], 1)
                return f

            def keep_h(b, u, i):
                dve.wait_ge(S["hs_out"], b + 1)
                dve.wait_ge(S["x1m"], b + 1)
                V.tensor_copy(nodes(b), hst[u].rearrange("p (n f) -> p n f", f=D)).then_inc(S["hs_acc"], 1)
            staged(dve, (0, relu_x, 4), (3, variance("z_sq", "z_sum2", "z_var"), 2), (1, centre("z", "z_sum", "z_cen"), 2),
                   (5, inverse("z_std", "z_rstd"), 2), (10, keep_h, 2))

            dve.wait_ge(S["hs_acc"], CHUNKS)
            for t in rows3:
                V.memset(t[:, :, D:], 0.0)
            V.memset(rel[0:1, 0, STEPS - 1:], float(WIN)).then_inc(S["p3_clear"], 1)
            for u in range(2):
                dve.wait_ge(s_hsst[u], 16 * uses(u))
            staged(dve, *steps_of(ph[1], 5), (2, low_part(ph[1], rows3, parts3), 2),
                   (1, after_high(ph[1], rows3, parts3), 2))
            late_sets(ph[1])

            dve.wait_ge(ph[1]["added"], STEPS)

            def negatives(b, u, i):
                dve.wait_ge(S["o_b"], b + 1)
                if not first(b):
                    dve.wait_ge(S["o_z"], b - 1)
                V.tensor_scalar(xds[u].rearrange("p (n f) -> p n f", f=D), nodes(b), 0.0, slo[:, 0:1], ALU.min, ALU.mult).then_inc(S["o_neg"], 1)

            def residual(b, u, i):
                dve.wait_ge(S["o_x"], b + 1)
                V.scalar_tensor_tensor(nodes(b), nodes(b), 0.0, xds[u].rearrange("p (n f) -> p n f", f=D), ALU.max, ALU.add).then_inc(S["o_z"], 1)

            staged(dve, (6, variance("o_sq", "o_sum2", "o_var"), 2), (4, residual, 2), (4, centre("o_z", "o_sum", "o_cen"), 2),
                   (2, negatives, 2), (7, inverse("o_std", "o_rstd"), 2))

        @block.tensor
        def _(pe):
            T = nc.tensor
            pe.wait_ge(S["src_ready"], 1)
            for bk, nm in ((2, "src"), (0, "dst"), (1, "nxt"), (3, "ew")):
                if nm == "dst":
                    last.then_inc(S["ppe0"], 1)
                    pe.wait_ge(S["cst16"], 1)
                for t in range(2):
                    for h in range(2):
                        o = (t * 2 + h) * HB
                        last = T.matmul(bank[bk][:, o:o + HB], nat[nm][:, h * BLK + t * P:h * BLK + (t + 1) * P], ident[0:HB, 0:HB],
                                 start=True, stop=True)
            for h in range(2):
                for hf in range(2):
                    T.matmul(bank[4][0:HB, h:h + 1], before[:, hf, h, :], cnt[:, hf:hf + 1], start=(hf == 0), stop=(hf == 1))
            T.matmul(bank[5][0:1, 0:1], crs, one, start=True, stop=True).then_inc(S["ppe1"], 1)
            pe.wait_ge(S["cst16"], 2)
            for t in range(2):
                for h in range(2):
                    T.matmul(bank[t][:, 0:STEPS], dadj[:, h * BLK + t * P:h * BLK + (t + 1) * P], oh[:, h, :], start=(h == 0), stop=(h == 1))
            for h in range(2):
                T.matmul(bank[4][0:1, 0:STEPS], fms[:, h:h + 1], oh[:, h, :], start=(h == 0), stop=(h == 1))
            for h in range(2):
                last = T.matmul(bank[5][0:1, 0:STEPS], order[:, h:h + 1], oh[:, h, :], start=(h == 0), stop=(h == 1))
            last.then_inc(S["ppe2"], 1)

            def steps(p, s, v, i, alone):
                for n in range(4):
                    k = 4 * s + n
                    pe.wait_ge(p["steprow"][4 * v + n], 16 * (i + 1))
                    pe.wait_ge(p["built"], k + 1)
                    if alone and not (isinstance(s, int) and s < EARLY + 2):
                        pe.wait_ge(p["moved"], k - 7 - 4 * EARLY)
                    elif alone:
                        pe.wait_ge(p["added"], 4 * EARLY)
                    elif not (isinstance(s, int) and s == 0):
                        pe.wait_ge(p["added"], k - 3)
                    u = uslot(n, v, alone)
                    cols = R if p is ph[0] else D
                    for q in range(Q):
                        for t in range(2):
                            for part in range(3):
                                last = T.matmul(u[:, q, 0:cols], onehot[:, n, t, q * P:(q + 1) * P], steprow[:, 4 * v + n, t, part, 0:cols],
                                                start=(t == 0 and part == 0), stop=(t == 1 and part == 2))
                    last.then_inc(p["mm"], 1)

            def early_sets(p):
                return lambda s, v, i: steps(p, s, v, i, False)

            def late_sets(p):
                pe.wait_ge(p["added"], 4 * EARLY)
                pe.wait_ge(p["rows_ready"], CHUNKS)
                for v in range(2):
                    steps(p, EARLY + v, v, EARLY // 2, True)
                with pe.Fori(EARLY // 2 + 1, SETS // 2) as i:
                    steps(p, 2 * i, 0, i, True)
                    steps(p, 2 * i + 1, 1, i, True)

            def transposes(c, u4, i):
                pe.wait_ge(s_gath[u4], 128 * (i + 1))
                u = u4 % 2
                if not first(c):
                    pe.wait_ge(S["exp_ready"], c - 1)
                if not first(c, 1):
                    pe.wait_ge(S["max_ready"], c)
                sel = spread[:, bass.ds(c, 1), :].rearrange("k c m -> k (c m)")
                T.matmul(n_p[:, :], sel, starts[0:2 * CHUNKS, :], start=True, stop=True)
                for n in range(4):
                    last = T.matmul(m_p[u][:, n * P:(n + 1) * P], g1[u4][:, n * P:(n + 1) * P], ident, start=(n == 0), stop=(n == 3),
                                    is_transpose=True, skip_group_check=True)
                last.then_inc(S["tr"], 1)

            def against_max(c, u, i):
                pe.wait_ge(S["max_ready"], c + 1)
                sel = spread[:, bass.ds(c, 1), :].rearrange("k c m -> k (c m)")
                T.matmul(m_p[u][:, :], sel, minus_starts[0:2 * CHUNKS, :], start=False, stop=False, skip_group_check=True)
                T.matmul(m_p[u][:, :], nident[:, :], run_max[u][:, 0:COLS], start=False, stop=True, skip_group_check=True).then_inc(S["z_ready"], 1)

            def product(c, u, i):
                pe.wait_ge(S["q_ready"], c + 1)
                if not first(c, 1):
                    pe.wait_ge(ph[0]["rows_ready"], c)
                for b in range(2):
                    for t in range(2):
                        o = (2 * b + t) * P
                        last = T.matmul(q_p[:, o:o + P], q1[u][:, o:o + P], w0[:, :], start=True, stop=True)
                last.then_inc(S["w_ready"], 1)

            pe.wait_ge(S["sources"], 1)
            pe.wait_ge(S["tables"], 1)
            pe.wait_ge(S["weights_d"], 16 * 7)
            staged(pe, (1, against_max, 2), (0, transposes, 4), (3, product, 2), (7, early_sets(ph[0]), 2, EARLY))
            pe.wait_ge(ph[0]["added"], 4 * EARLY)
            pe.wait_ge(S["sum_ready"], CHUNKS)
            T.matmul(bank[7][:, 400:403], shift, msa[0][:, :, COLS], start=True, stop=True).then_inc(S["fix_pe"], 1)
            pe.wait_ge(S["fix_q"], 2)
            T.matmul(bank[7][0:1, 0:P], fixs[:, 11:12], w0[:, :], start=True, stop=True).then_inc(S["fix_pe"], 1)
            pe.wait_ge(S["fix_row"], 1)
            late_sets(ph[0])

            pe.wait_ge(ph[0]["added"], STEPS)

            def transpose2(b, u4, i):
                pe.wait_ge(S["x1m"], b + 1)
                if not first(b):
                    pe.wait_ge(S["x1_tc"], b - 1)
                for w in range(4):
                    last = T.matmul(m_p[u4 % 2][:, w * P:(w + 1) * P], x1s[u4][:, w * P:(w + 1) * P], ident, start=True, stop=True, is_transpose=True)
                last.then_inc(S["x1_t"], 1)

            def product2(b, u, i):
                pe.wait_ge(S["x1_tc"], b + 1)
                if not first(b):
                    pe.wait_ge(S["hs_out"], b - 1)
                for w in range(4):
                    last = T.matmul(h_p[u][:, w * P:(w + 1) * P], xdt[u][:, w * P:(w + 1) * P], w1[:, :], start=True, stop=True)
                last.then_inc(S["hsp"], 1)
            staged(pe, (7, transpose2, 4), (8, product2, 2))

            pe.wait_ge(S["hs_acc"], CHUNKS)
            staged(pe, (5, early_sets(ph[1]), 2, EARLY))
            late_sets(ph[1])


def kernel(x, src, dst, edge_attr_64, edge_weight, L0_gnn_W, L0_gnn_b, L1_gnn_W, L1_gnn_bias, L1_gnn_prelu_w):
    import concourse.bacc as bacc
    from concourse.bass_utils import run_bass_kernel_spmd

    kept, setup = constants()
    arrays = {
        "x": np.asarray(x), "src": np.asarray(src), "dst": np.asarray(dst),
        "ef": np.asarray(edge_attr_64), "ew": np.asarray(edge_weight),
        "w0t": np.ascontiguousarray(np.asarray(L0_gnn_W).T), "b0": np.asarray(L0_gnn_b),
        "w1t": np.ascontiguousarray(np.asarray(L1_gnn_W).T), "b1": np.asarray(L1_gnn_bias),
        "slope": np.asarray(L1_gnn_prelu_w).reshape(1, 1), "kept": kept, "setup": setup,
    }
    nc = bacc.Bacc("TRN2", target_bir_lowering=False, num_devices=1)
    args = [nc.dram_tensor("in_" + n, a.shape, mybir.dt.from_np(a.dtype), kind="ExternalInput").ap() for n, a in arrays.items()]
    args.append(nc.dram_tensor("out_0", (N, D), F32, kind="ExternalOutput").ap())
    for n, shape in (("rows", ((NB + 1) * P, 2 * 3 * R)), ("x1", (P * NODES, D)), ("hs", (P * NODES, D))):
        args.append(nc.dram_tensor(n + "_dram", shape, BF16 if n == "rows" else F32, kind="Internal").ap())
    gnn_kernel(nc, *args)
    r = run_bass_kernel_spmd(nc, [{"in_" + n: a for n, a in arrays.items()}], core_ids=[0])
    return r.results[0]["out_0"]
```
